# Optimizing a Trainium2 kernel written in Bass

```python
import numpy as np
import jax
import jax.numpy as jnp

def _softmax(x, axis=-1):
    return jax.nn.softmax(x, axis=axis)

def _gelu(x):
    return jax.nn.gelu(x, approximate=True)

def _silu(x):
    return jax.nn.silu(x)

def _sigmoid(x):
    return jax.nn.sigmoid(x)

def _layernorm(x, axis=-1, eps=1e-05):
    m = jnp.mean(x, axis=axis, keepdims=True)
    v = jnp.var(x, axis=axis, keepdims=True)
    return (x - m) / jnp.sqrt(v + eps)

def _scatter_add(tgt, idx, src, axis=0):
    return tgt.at[idx].add(src)

def _segment_sum(src, seg, n):
    return jax.ops.segment_sum(src, seg, n)
kernel_name = 'mk_gnn_ffn_d1_gnn_r64_720781'

def setup_inputs(seed: int=0):
    np.random.seed(seed)
    _w = jnp.asarray

    def _rec_inputs():
        import jax
        import jax.numpy as jnp
        _gk = jax.random.key(seed)
        x = -0.0003929 + 0.9999 * jax.random.normal(jax.random.fold_in(_gk, 1), (256, 1024), jnp.float32)
        src = jax.random.randint(jax.random.fold_in(_gk, 2), (8192,), 0, 256, jnp.int32)
        dst = jnp.minimum((256 * jax.random.uniform(jax.random.fold_in(_gk, 3), (8192,)) ** 2.0).astype(jnp.int32), 16383)
        _o = jnp.argsort(dst, stable=True)
        src = src[_o]
        dst = dst[_o]
        return (x, src, dst)
    x, src, dst = _rec_inputs()

    def _L0_gnn_setup():
        import jax, jax.numpy as jnp
        import numpy as np
        NH, NO = (64, 192)
        N = NH + NO
        E_HH, E_OO, E_HO = (128, 640, 256)
        E = E_HH + E_OO + E_HO
        D = 1024
        key = jax.random.key(seed)
        ks = jax.random.split(key, 12)
        w = lambda k, s: jax.random.normal(k, s, jnp.float32) * 0.02
        return {'n_f': jax.random.normal(ks[0], (N, D), jnp.float32), 'W_hh': w(ks[1], (2 * D, D)), 'b_hh': jnp.zeros((D,), jnp.float32), 'W_oo': w(ks[2], (2 * D, D)), 'b_oo': jnp.zeros((D,), jnp.float32), 'W_ho': w(ks[3], (2 * D, D)), 'b_ho': jnp.zeros((D,), jnp.float32), 'W_a': w(ks[4], (D, 1)), 'b_a': jnp.zeros((1,), jnp.float32), 'W_hn': w(ks[5], (2 * D, D)), 'b_hn': jnp.zeros((D,), jnp.float32), 'W_on': w(ks[6], (2 * D, D)), 'b_on': jnp.zeros((D,), jnp.float32), 'edge_src': jax.random.randint(ks[7], (E,), 0, N, jnp.int32), 'edge_dst': jax.random.randint(ks[8], (E,), 0, N, jnp.int32)}
    _L0_gnn_all = _L0_gnn_setup()
    _L0_gnn_in = {k: v for k, v in _L0_gnn_all.items() if k in ('W_hh', 'b_hh', 'W_oo', 'b_oo', 'W_ho', 'b_ho', 'W_a', 'b_a', 'W_hn', 'b_hn', 'W_on', 'b_on')}
    del _L0_gnn_all

    def _L0_ffn_setup():
        import jax, jax.numpy as jnp
        import numpy as np
        TOP_K = 4
        key = jax.random.key(seed)
        ks = jax.random.split(key, 5)
        B, T, D = (2, 1024, 1024)
        P, PD = (256, 32)
        return {'x': jax.random.normal(ks[0], (B, T, D), dtype=jnp.float32), 'hasher_w': jax.random.normal(ks[1], (PD, D), dtype=jnp.float32) * 0.03, 'keys': jax.random.normal(ks[2], (P, PD), dtype=jnp.float32) * 0.1, 'values_down': jax.random.normal(ks[3], (P, D, PD), dtype=jnp.float32) * 0.01, 'values_up': jax.random.normal(ks[4], (P, PD, D), dtype=jnp.float32) * 0.01, 'scale': jnp.full((1,), 0.1, dtype=jnp.float32)}
    _L0_ffn_all = _L0_ffn_setup()
    _L0_ffn_in = {k: v for k, v in _L0_ffn_all.items() if k in ('hasher_w', 'keys', 'values_down', 'values_up', 'scale')}
    del _L0_ffn_all
    return {'x': x, 'src': src, 'dst': dst, 'L0_gnn_W_hh': _L0_gnn_in['W_hh'], 'L0_gnn_b_hh': _L0_gnn_in['b_hh'], 'L0_gnn_W_oo': _L0_gnn_in['W_oo'], 'L0_gnn_b_oo': _L0_gnn_in['b_oo'], 'L0_gnn_W_ho': _L0_gnn_in['W_ho'], 'L0_gnn_b_ho': _L0_gnn_in['b_ho'], 'L0_gnn_W_a': _L0_gnn_in['W_a'], 'L0_gnn_b_a': _L0_gnn_in['b_a'], 'L0_gnn_W_hn': _L0_gnn_in['W_hn'], 'L0_gnn_b_hn': _L0_gnn_in['b_hn'], 'L0_gnn_W_on': _L0_gnn_in['W_on'], 'L0_gnn_b_on': _L0_gnn_in['b_on'], 'L0_ffn_hasher_w': _L0_ffn_in['hasher_w'], 'L0_ffn_keys': _L0_ffn_in['keys'], 'L0_ffn_values_down': _L0_ffn_in['values_down'], 'L0_ffn_values_up': _L0_ffn_in['values_up'], 'L0_ffn_scale': _L0_ffn_in['scale']}

def reference(x, src, dst, L0_gnn_W_hh, L0_gnn_b_hh, L0_gnn_W_oo, L0_gnn_b_oo, L0_gnn_W_ho, L0_gnn_b_ho, L0_gnn_W_a, L0_gnn_b_a, L0_gnn_W_hn, L0_gnn_b_hn, L0_gnn_W_on, L0_gnn_b_on, L0_ffn_hasher_w, L0_ffn_keys, L0_ffn_values_down, L0_ffn_values_up, L0_ffn_scale):
    import jax
    import jax.numpy as jnp

    def _L0_gnn_ref(n_f, W_hh, b_hh, W_oo, b_oo, W_ho, b_ho, W_a, b_a, W_hn, b_hn, W_on, b_on, edge_src, edge_dst):
        import jax, jax.numpy as jnp
        import numpy as np
        NH, NO = (64, 192)
        N = NH + NO
        E_HH, E_OO, E_HO = (128, 640, 256)
        E = E_HH + E_OO + E_HO
        D = 1024
        feat = jnp.concatenate([n_f[edge_src], n_f[edge_dst]], axis=1)
        e_hh = jax.nn.relu(feat[:E_HH] @ W_hh + b_hh)
        e_oo = jax.nn.relu(feat[E_HH:E_HH + E_OO] @ W_oo + b_oo)
        e_ho = jax.nn.relu(feat[E_HH + E_OO:] @ W_ho + b_ho)
        e_f = jnp.concatenate([e_hh, e_oo, e_ho], axis=0)
        logit = (e_f @ W_a + b_a)[:, 0]
        m = jax.lax.stop_gradient(jax.ops.segment_max(logit, edge_dst, num_segments=N))
        ex = jnp.exp(logit - m[edge_dst])
        den = jax.ops.segment_sum(ex, edge_dst, num_segments=N)
        alpha = ex / den[edge_dst]
        z_f = jax.ops.segment_sum(alpha[:, None] * n_f[edge_src], edge_dst, num_segments=N)
        nf2 = jnp.concatenate([n_f, z_f], axis=1)
        h_new = jax.nn.relu(nf2[:NH] @ W_hn + b_hn)
        o_new = jax.nn.relu(nf2[NH:] @ W_on + b_on)
        return jnp.concatenate([h_new, o_new], axis=0)

    def _L0_ffn_ref(x, hasher_w, keys, values_down, values_up, scale):
        import jax, jax.numpy as jnp
        import numpy as np
        TOP_K = 4
        h = jnp.einsum('btd,pd->btp', x, hasher_w)
        sim = jnp.einsum('btp,np->btn', h, keys)
        vals, idx = jax.lax.top_k(sim, TOP_K)
        w = jax.nn.softmax(vals, axis=-1)
        out = jnp.zeros_like(x)
        for k in range(TOP_K):
            ik = idx[..., k]
            vd = values_down[ik]
            vu = values_up[ik]
            proj = jax.nn.silu(jnp.einsum('btd,btdp->btp', x, vd))
            o = jnp.einsum('btp,btpd->btd', proj, vu)
            out = out + o * w[..., k:k + 1]
        return x + out * scale
    x = x + _L0_gnn_ref(_layernorm(x, axis=-1), L0_gnn_W_hh, L0_gnn_b_hh, L0_gnn_W_oo, L0_gnn_b_oo, L0_gnn_W_ho, L0_gnn_b_ho, L0_gnn_W_a, L0_gnn_b_a, L0_gnn_W_hn, L0_gnn_b_hn, L0_gnn_W_on, L0_gnn_b_on, src, dst)
    x = x + _L0_ffn_ref(_layernorm(x, axis=-1)[None], L0_ffn_hasher_w, L0_ffn_keys, L0_ffn_values_down, L0_ffn_values_up, L0_ffn_scale)[0]
    return x

_drawn_inputs = setup_inputs


def setup_inputs(seed=0):
    import zlib

    import numpy as np

    out = dict(_drawn_inputs(seed))
    spreads = {'L0_gnn_b_hh': (0.0, 2.0),
     'L0_gnn_b_oo': (0.0, 2.0),
     'L0_gnn_b_ho': (0.0, 2.0),
     'L0_gnn_b_hn': (0.0, 0.1),
     'L0_gnn_b_on': (0.0, 0.1)}
    factors = {'L0_gnn_W_hh': 64.0,
     'L0_gnn_W_oo': 40.526,
     'L0_ffn_hasher_w': 8.0,
     'L0_ffn_keys': 8.0,
     'L0_ffn_values_down': 8.0,
     'L0_ffn_values_up': 8.0}
    for name, (base, spread) in spreads.items():
        noise = np.random.default_rng([zlib.crc32(name.encode()), seed]).standard_normal(out[name].shape)
        drawn = base * np.exp(spread * noise) if base else spread * noise
        out[name] = jnp.asarray(drawn.astype(out[name].dtype))
    for name, factor in factors.items():
        out[name] = (out[name] * factor).astype(out[name].dtype)
    return out
```

```python
from contextlib import ExitStack

import concourse.bass as bass
from concourse import mybir
from concourse.alu_op_type import AluOpType as ALU

F32 = mybir.dt.float32
F32R = mybir.dt.float32r
BF16 = mybir.dt.bfloat16
I32 = mybir.dt.int32
U32 = mybir.dt.uint32
ACT = mybir.ActivationFunctionType
RMAX = bass.bass_isa.ReduceOp.max

P = 128
N = 256
NT = N // P
D = 1024
C = D // P
HALF = 512
NH = 64
PADN = N + 2 * NH
PADZ = N + NH
E = 8192
ET = E // P
FIRST_TILE = [0, 1, 6, ET]
BATCH = 2 * P
NB = E // BATCH
XP = 256
PD = 32
TOPK = 4
GX = 16
NG = XP // GX
UNIT = 4096
WUNITS = 20
SLOT_W = WUNITS // 2
EPS = 1e-5
NEVER = -3.0e38
BLOCKS = GX * PD // P


def gnn_ffn(nc, x, src, dst, W_hh, b_hh, W_oo, b_oo, W_ho, b_ho, W_a, b_a, W_hn, b_hn, W_on, b_on,
            hasher_w, keys, values_down, values_up, scale, out):
    ctx = ExitStack()
    with ctx:
        def sb(name, shape, dt=F32, where=ctx):
            return where.enter_context(nc.sbuf_tensor(name, shape, dt))

        def sem(name):
            return ctx.enter_context(nc.semaphore(name))

        raw = sb("raw", [P, 2, UNIT])
        whi = sb("whi", [P, 2, UNIT], F32R)
        wlo = sb("wlo", [P, 2, UNIT], F32R)
        xt = sb("xt", [P, NT, D])
        nf = sb("nf", [P, NT, D])
        nT_hi = sb("nT_hi", [P, C, PADN], F32R)
        nT_lo = sb("nT_lo", [P, C, PADN], F32R)
        iota = sb("iota", [P, N])
        node = sb("node", [P, 2])
        ident = sb("ident", [P, P])
        ones = sb("ones", [P, P])
        sel = sb("sel", [5, 5, P])
        bias = sb("bias", [5, D])
        segmax = sb("segmax", [P, N])
        segall = sb("segall", [P, N])
        logit = sb("logit", [P, ET])
        peak = sb("peak", [P, ET])
        ex = sb("ex", [P, ET])
        ex_hi = sb("ex_hi", [P, ET], F32R)
        ex_lo = sb("ex_lo", [P, ET])
        idx_col = sb("idx_col", [P, 2, ET])
        hash_hi = sb("hash_hi", [P, C, PD], F32R)
        hash_lo = sb("hash_lo", [P, C, PD], F32R)
        keysT = sb("keysT", [PD, XP])
        scale_b = sb("scale_b", [P, 1])
        ba_b = sb("ba_b", [P, 1])
        stats = sb("stats", [P, NT, 2, 6])
        mv = sb("mv", [P, NT, 2])
        ln = sb("ln", [P, 6, NT])
        with ExitStack() as early:
            idx_rows = sb("idx_rows", [ET, 2, P], I32, early)
            idx_rowf = sb("idx_rowf", [ET, 2, P], F32, early)
            hash_w = sb("hash_w", [PD, D], F32, early)
            keys_n = sb("keys_n", [P, NT, PD], F32, early)
        with ExitStack() as edge:
            tab_hi = sb("tab_hi", [P, 4, D], F32R, edge)
            tab_lo = sb("tab_lo", [P, 4, D], F32R, edge)
            onehot = sb("onehot", [P, 2, 4, BATCH], F32R, edge)
            idx_b = sb("idx_b", [P, 2, 2, BATCH], I32, edge)
            wa_b = sb("wa_b", [P, D], F32, edge)
            junk = sb("junk", [P, D], BF16, edge)
            pen = sb("pen", [P, N], F32, edge)
        with ExitStack() as late:
            zT_hi = sb("zT_hi", [P, C, PADZ], F32R, late)
            zT_lo = sb("zT_lo", [P, C, PADZ], F32R, late)
            junk2 = sb("junk2", [P, 2, N], F32, late)
            oh_src = sb("oh_src", [P, 2, N], F32R, late)
            oh_dst = sb("oh_dst", [P, 2, 2, N], F32R, late)
            pT = sb("pT", [P, NT, N], F32, late)
            rden = sb("rden", [P, N], F32, late)
        h_sb = sb("h_sb", [P, NT, PD])
        hT_sb = sb("hT_sb", [PD, N])
        sim = sb("sim", [P, NT, XP])
        top = sb("top", [P, NT, 8])
        topi = sb("topi", [P, NT, 8], U32)
        topf = sb("topf", [P, NT, 8])
        tope = sb("tope", [P, NT, 8])
        tsum = sb("tsum", [P, NT, 2])
        route = sb("route", [P, NT, XP])
        rtmp = sb("rtmp", [P, 2, XP])
        act_g = sb("act_g", [P, NT, GX * PD])
        gw = sb("gw", [P, NT, GX * PD])
        gT_hi = sb("gT_hi", [P, BLOCKS, N], F32R)
        gT_lo = sb("gT_lo", [P, BLOCKS, N], F32R)

        ps = ctx.enter_context(nc.psum_tensor("ps", [P, 8 * HALF], F32))

        def bank(b, n=1):
            return ps[:, b * HALF:(b + n) * HALF]

        low_cn = bank(0, 4).rearrange("p (c n) -> p c n", c=C)
        high_cn = bank(4, 4).rearrange("p (c n) -> p c n", c=C)

        x_loaded = sem("x_loaded")
        idx_loaded = sem("idx_loaded")
        small_loaded = sem("small_loaded")
        edge_loaded = sem("edge_loaded")
        batch_loaded = [sem(f"batch_loaded{s}") for s in range(2)]
        loaded = [sem(f"loaded{s}") for s in range(2)]
        hi_ready = [sem(f"hi_ready{s}") for s in range(2)]
        lo_ready = [sem(f"lo_ready{s}") for s in range(2)]
        used = [sem(f"used{s}") for s in range(2)]
        consts = sem("consts")
        pool_chain = sem("pool_chain")
        chain = sem("chain")
        var_ready = sem("var_ready")
        root_ready = sem("root_ready")
        norm_ready = sem("norm_ready")
        turned = sem("turned")
        turned_hi = sem("turned_hi")
        turned_lo = sem("turned_lo")
        idx_float = sem("idx_float")
        smallT = sem("smallT")
        hash_ready = sem("hash_ready")
        small_ready = sem("small_ready")
        biased = sem("biased")
        tabhi_ready = sem("tabhi_ready")
        tablo_ready = sem("tablo_ready")
        onehot_ready = sem("onehot_ready")
        gathered = sem("gathered")
        pen_ready = sem("pen_ready")
        dot_done = sem("dot_done")
        seg_done = sem("seg_done")
        segall_ready = sem("segall_ready")
        peak_done = sem("peak_done")
        diff_ready = sem("diff_ready")
        ex_ready = sem("ex_ready")
        exlo_ready = sem("exlo_ready")
        ohsrc_ready = sem("ohsrc_ready")
        ohdst_ready = sem("ohdst_ready")
        paired = sem("paired")
        pT_ready = sem("pT_ready")
        den_ready = sem("den_ready")
        pTn_ready = sem("pTn_ready")
        z_ready = sem("z_ready")
        zhi_ready = sem("zhi_ready")
        zlo_ready = sem("zlo_ready")
        x2_ready = sem("x2_ready")
        h_done = sem("h_done")
        h_copied = sem("h_copied")
        hT_done = sem("hT_done")
        hT_copied = sem("hT_copied")
        sim_done = sem("sim_done")
        top_ready = sem("top_ready")
        tope_ready = sem("tope_ready")
        silu_ready = sem("silu_ready")
        gw_ready = sem("gw_ready")
        gT_done = sem("gT_done")
        gThi_ready = sem("gThi_ready")
        gTlo_ready = sem("gTlo_ready")
        out_ready = sem("out_ready")
        stored = sem("stored")

        def rows(w, half, quarter):
            v = w[half * D:(half + 1) * D, :].rearrange("(p c) n -> p c n", c=C)
            return v[:, 4 * quarter:4 * quarter + 4, :]

        unit_source = [rows(w, h, q) for w in (W_hh, W_oo, W_ho) for h in range(2) for q in range(2)]
        unit_source += [rows(w, h, q) for h in range(2) for w in (W_hn, W_on) for q in range(2)]
        down_v = values_down.rearrange("n (p c) w -> p n (c w)", c=C)
        up_v = values_up.rearrange("n w d -> (n w) d").rearrange("(b q) d -> q b d", q=P)
        raw_down = raw[:, 0, :].rearrange("p (n k) -> p n k", n=GX)
        raw_up = raw[:, 1, :].rearrange("p (b d) -> p b d", b=BLOCKS)

        def tokens(t3, c, t):
            return t3[:, c, NH:NH + P] if t == 0 else t3[:, c, 4 * NH:PADN]

        def token_columns(k):
            if k == 0:
                return (NH, NH, NH), (2 * NH, 0, NH), (4 * NH, P, P)
            return (NH, 0, P), (4 * NH, P, P)

        block = ctx.enter_context(nc.Block())

        @block.sync
        def _(sp):
            for u in range(WUNITS):
                s, n = u % 2, u // 2
                if n:
                    sp.wait_ge(lo_ready[s], n)
                dst_ap = raw[:, s, :].rearrange("p (c n) -> p c n", c=4)
                sp.dma_start(dst_ap, unit_source[u]).then_inc(loaded[s], 16)
            sp.wait_ge(lo_ready[0], SLOT_W)
            sp.dma_start(raw_down, down_v[:, 0:GX, :]).then_inc(loaded[0], 16)
            with sp.Fori(0, NG - 1) as g:
                sp.wait_ge(lo_ready[0], SLOT_W + 1 + g)
                sp.dma_start(raw_down, down_v[:, bass.ds((g + 1) * GX, GX), :]).then_inc(loaded[0], 16)
                sp.wait_ge(lo_ready[1], SLOT_W + g)
                sp.dma_start(raw_up, up_v[:, bass.ds(g * BLOCKS, BLOCKS), :]).then_inc(loaded[1], 16)
            sp.wait_ge(lo_ready[1], SLOT_W + NG - 1)
            sp.dma_start(raw_up, up_v[:, (NG - 1) * BLOCKS:NG * BLOCKS, :]).then_inc(loaded[1], 16)
            out_v = out.rearrange("(t p) n -> p t n", p=P)
            for t in range(NT):
                sp.wait_ge(out_ready, t + 1)
                sp.dma_start(out_v[:, t, :], xt[:, t, :]).then_inc(stored, 16)
            sp.wait_ge(stored, 16 * NT)

        @block.gpsimd
        def _(pool):
            made = [0]

            def constant(ins):
                made[0] += 1
                ins.then_inc(consts, 1)
                pool.wait_ge(consts, made[0])

            nc.gpsimd.memset(ident[:], 0.0).then_inc(pool_chain, 1)
            nc.gpsimd.memset(sel[:], 1.0).then_inc(pool_chain, 1)
            pool.wait_ge(pool_chain, 2)
            constant(nc.gpsimd.affine_select(out=ident[:], in_=ident[:], compare_op=ALU.not_equal, fill=1.0,
                                             base=0, pattern=[[-1, P]], channel_multiplier=1))
            constant(nc.gpsimd.affine_select(out=sel[:], in_=sel[:], compare_op=ALU.is_equal, fill=0.0,
                                             base=0, pattern=[[-1, 5], [0, P]], channel_multiplier=1))
            for T in (nT_hi, nT_lo):
                for at in (0, 3 * NH):
                    constant(nc.gpsimd.memset(T[:, :, at:at + NH].bitcast(F32), 0.0))
            for col, part, base in ((0, 0, NH), (0, NH, 0), (1, 0, P), (1, NH, P + NH)):
                constant(nc.gpsimd.iota(node[part:part + NH, col:col + 1], pattern=[[0, 1]], base=base,
                                        channel_multiplier=1, allow_small_or_imprecise_dtypes=True))
            constant(nc.gpsimd.iota(iota[:], pattern=[[1, N]], base=0, channel_multiplier=0,
                                    allow_small_or_imprecise_dtypes=True))
            constant(nc.gpsimd.memset(ones[:], 1.0))
            constant(nc.gpsimd.memset(segmax[:], NEVER))

            def load_batch(b, s):
                pool.dma_start(idx_b[:, s, 0, :], src[bass.ds(b * BATCH, BATCH)].partition_broadcast(P))\
                    .then_inc(batch_loaded[s], 16)
                pool.dma_start(idx_b[:, s, 1, :], dst[bass.ds(b * BATCH, BATCH)].partition_broadcast(P))\
                    .then_inc(batch_loaded[s], 16)

            load_batch(0, 0)
            load_batch(1, 1)
            with pool.Fori(1, NB // 2) as i:
                for s in range(2):
                    pool.wait_ge(onehot_ready, 2 * i - 1 + s)
                    load_batch(2 * i + s, s)

            pool.wait_ge(seg_done, ET)
            nc.gpsimd.partition_all_reduce(segall[:], segmax[:], P, RMAX).then_inc(segall_ready, 1)
            pool.wait_ge(gathered, ET)
            nc.gpsimd.memset(zT_hi[:, :, NH:2 * NH].bitcast(F32), 0.0).then_inc(pool_chain, 1)
            nc.gpsimd.memset(zT_lo[:, :, NH:2 * NH].bitcast(F32), 0.0).then_inc(pool_chain, 1)

            for i in range(ET):
                if i >= 2:
                    pool.wait_ge(paired, i - 1)
                nc.gpsimd.tensor_scalar(oh_src[:, i % 2, :], iota[:], idx_col[:, 0, i:i + 1], None,
                                        ALU.is_equal).then_inc(ohsrc_ready, 1)

        @block.scalar
        def _(act):
            x_v = x.rearrange("(t p) n -> p t n", p=P)
            for t in range(NT):
                act.dma_start(xt[:, t, :], x_v[:, t, :]).then_inc(x_loaded, 16)
            act.dma_start(idx_rows[:, 0, :], src.rearrange("(t p) -> t p", p=P)).then_inc(idx_loaded, 16)
            act.dma_start(idx_rows[:, 1, :], dst.rearrange("(t p) -> t p", p=P)).then_inc(idx_loaded, 16)
            act.dma_start(hash_w[:], hasher_w).then_inc(small_loaded, 16)
            act.dma_start(keys_n[:], keys.rearrange("(t p) w -> p t w", p=P)).then_inc(small_loaded, 16)
            for q, b in enumerate((b_hh, b_oo, b_ho, b_hn, b_on)):
                act.dma_start(bias[q:q + 1, :], b.rearrange("(a n) -> a n", a=1)).then_inc(small_loaded, 16)
            act.dma_start(scale_b[:], scale.partition_broadcast(P)).then_inc(small_loaded, 16)
            act.dma_start(wa_b[:], W_a.rearrange("n a -> (n a)").partition_broadcast(P)).then_inc(edge_loaded, 16)
            act.dma_start(ba_b[:], b_a.partition_broadcast(P)).then_inc(edge_loaded, 16)

            def root(k):
                act.wait_ge(var_ready, k + 1)
                nc.scalar.activation(ln[:, 1, :], ln[:, 0, :], ACT.Sqrt).then_inc(root_ready, 1)

            def turn_hi(k):
                act.wait_ge(turned, k + 1)
                for to, at, w in token_columns(k):
                    last = nc.scalar.activation(nT_hi[:, :, to:to + w], high_cn[:, :, at:at + w], ACT.Copy)
                last.then_inc(turned_hi, 1)

            def hi(s, n, first=False):
                act.wait_ge(loaded[s], 16 * (n + 1))
                if not first:
                    act.wait_ge(used[s], n)
                nc.scalar.activation(whi[:, s, :], raw[:, s, :], ACT.Copy).then_inc(hi_ready[s], 1)

            root(0)
            hi(0, 0, first=True)
            turn_hi(0)
            act.wait_ge(smallT, 1)
            nc.scalar.activation(hash_hi[:], bank(1)[:, 0:C * PD].rearrange("p (c w) -> p c w", c=C), ACT.Copy)\
                .then_inc(hash_ready, 1)

            def table_hi(k, h):
                if h == 0:
                    act.wait_ge(used[1], 2 * k + 1)
                else:
                    act.wait_ge(biased, k + 1)
                if k:
                    act.wait_ge(gathered, FIRST_TILE[k])
                nc.scalar.activation(tab_hi[:, 2 * h:2 * h + 2, :].rearrange("p t n -> p (t n)"),
                                     bank(4 * h, 4), ACT.Copy).then_inc(tabhi_ready, 1)

            for k in range(3):
                hi(1, 2 * k, first=k == 0)
                hi(0, 2 * k + 1)
                table_hi(k, 0)
                hi(1, 2 * k + 1)
                hi(0, 2 * k + 2)
                table_hi(k, 1)
            hi(1, 6)
            hi(0, 7)
            hi(1, 7)
            act.wait_ge(diff_ready, 1)
            nc.scalar.activation(ex[:], peak[:], ACT.Exp).then_inc(ex_ready, 1)
            act.wait_ge(ex_ready, 1)
            nc.scalar.activation(ex_hi[:], ex[:], ACT.Copy).then_inc(ex_ready, 1)
            hi(0, 8)
            hi(1, 8)
            act.wait_ge(paired, ET)
            nc.scalar.activation(pT[:], bank(4, 2).rearrange("p (t n) -> p t n", t=NT)[:, :, 0:N], ACT.Copy)\
                .then_inc(pT_ready, 1)
            act.wait_ge(z_ready, 1)
            nc.scalar.activation(zT_hi[:, :, 0:NH], high_cn[:, :, 0:NH], ACT.Copy)
            nc.scalar.activation(zT_hi[:, :, 2 * NH:PADZ], high_cn[:, :, NH:N], ACT.Copy).then_inc(zhi_ready, 1)
            hi(0, 9)
            hi(1, 9)
            hi(0, SLOT_W)
            root(1)
            turn_hi(1)
            act.wait_ge(top_ready, 1)
            for t in range(NT):
                nc.scalar.activation(tope[:, t, 0:TOPK], tope[:, t, TOPK:2 * TOPK], ACT.Exp,
                                     accum_out=tsum[:, t, 0:1]).then_inc(tope_ready, 1)

            d_cols = bank(4, 2)
            t_cols = bank(6, 2)

            def silu(g):
                act.wait_ge(used[0], g + (SLOT_W + 1))
                nc.scalar.activation(act_g[:].rearrange("p t n -> p (t n)"), d_cols, ACT.Silu)\
                    .then_inc(silu_ready, 1)

            def gT_hi_part(g):
                act.wait_ge(gT_done, g + 1)
                nc.scalar.activation(gT_hi[:].rearrange("p b n -> p (b n)"), t_cols, ACT.Copy)\
                    .then_inc(gThi_ready, 1)

            silu(0)
            hi(0, SLOT_W + 1)
            hi(1, SLOT_W)
            with act.Fori(1, NG - 1) as g:
                gT_hi_part(g - 1)
                silu(g)
                hi(0, SLOT_W + 1 + g)
                hi(1, SLOT_W + g)
            gT_hi_part(NG - 2)
            silu(NG - 1)
            hi(1, SLOT_W + NG - 1)
            gT_hi_part(NG - 1)

        @block.vector
        def _(dve):
            links = [0]

            def link(ins):
                links[0] += 1
                ins.then_inc(chain, 1)
                dve.wait_ge(chain, links[0])

            def lo(s, n):
                dve.wait_ge(hi_ready[s], n + 1)
                nc.vector.tensor_tensor(wlo[:, s, :], raw[:, s, :], whi[:, s, :].bitcast(F32), ALU.subtract)\
                    .then_inc(lo_ready[s], 1)

            def layer_norm(k):
                for t in range(NT):
                    if k == 0:
                        dve.wait_ge(x_loaded, 16 * NT)
                    for j in range(2):
                        last = nc.vector.bn_stats(stats[:, t, j, :], xt[:, t, j * HALF:(j + 1) * HALF])
                link(last)
                for t in range(NT):
                    last = nc.vector.bn_aggr(mv[:, t, :], stats[:, t, :, :].rearrange("p j s -> p (j s)"))
                link(last)
                nc.vector.tensor_scalar(ln[:, 0, :], mv[:, :, 1], EPS, None, ALU.add).then_inc(var_ready, 1)
                dve.wait_ge(root_ready, k + 1)
                link(nc.vector.reciprocal(ln[:, 2, :], ln[:, 1, :]))
                link(nc.vector.tensor_tensor(ln[:, 3, :], ln[:, 0, :], ln[:, 2, :], ALU.mult))
                link(nc.vector.tensor_tensor(ln[:, 4, :], ln[:, 3, :], ln[:, 1, :], ALU.add))
                link(nc.vector.tensor_scalar(ln[:, 3, :], ln[:, 4, :], 0.5, None, ALU.mult))
                link(nc.vector.reciprocal(ln[:, 5, :], ln[:, 3, :]))
                for t in range(NT):
                    nc.vector.tensor_scalar(nf[:, t, :], xt[:, t, :], mv[:, t, 0:1], ln[:, 5, t:t + 1],
                                            ALU.subtract, ALU.mult).then_inc(norm_ready, 1)

            def turn_lo(k):
                dve.wait_ge(turned_hi, k + 1)
                for to, at, w in token_columns(k):
                    last = nc.vector.tensor_tensor(nT_lo[:, :, to:to + w], high_cn[:, :, at:at + w],
                                                   nT_hi[:, :, to:to + w].bitcast(F32), ALU.subtract)
                last.then_inc(turned_lo, 1)

            layer_norm(0)
            dve.wait_ge(idx_loaded, 32)
            nc.vector.tensor_copy(idx_rowf[:], idx_rows[:]).then_inc(idx_float, 1)
            turn_lo(0)
            lo(0, 0)
            dve.wait_ge(hash_ready, 1)
            nc.vector.tensor_tensor(hash_lo[:], bank(1)[:, 0:C * PD].rearrange("p (c w) -> p c w", c=C),
                                    hash_hi[:].bitcast(F32), ALU.subtract)
            nc.vector.tensor_copy(idx_col[:].rearrange("p a t -> p (a t)"), bank(0)[:, 0:2 * ET])
            nc.vector.tensor_copy(keysT[:], bank(2)[0:PD, 0:XP]).then_inc(small_ready, 1)

            def table_lo(k, h):
                dve.wait_ge(tabhi_ready, 2 * k + h + 1)
                nc.vector.tensor_tensor(tab_lo[:, 2 * h:2 * h + 2, :].rearrange("p t n -> p (t n)"),
                                        bank(4 * h, 4),
                                        tab_hi[:, 2 * h:2 * h + 2, :].rearrange("p t n -> p (t n)").bitcast(F32),
                                        ALU.subtract).then_inc(tablo_ready, 1)

            def make_onehot(b, s, free=True):
                dve.wait_ge(batch_loaded[s], 32 * (b // 2 + 1))
                if free:
                    dve.wait_ge(gathered, 2 * b - 2)
                for a in range(2):
                    for j in range(2):
                        last = nc.vector.tensor_scalar(onehot[:, s, 2 * a + j, :], idx_b[:, s, a, :],
                                                       node[:, j:j + 1], None, ALU.is_equal)
                last.then_inc(onehot_ready, 1)

            def edge_tile(i, q):
                dve.wait_ge(gathered, i + 1)
                nc.vector.scalar_tensor_tensor(out=junk[:], in0=bank(2 * q, 2), scalar=0.0, in1=wa_b[:],
                                               op0=ALU.max, op1=ALU.mult,
                                               accum_out=logit[:, bass.ds(i, 1)]).then_inc(dot_done, 1)
                if not isinstance(i, int) or i:
                    dve.wait_ge(seg_done, i)
                nc.vector.tensor_scalar(pen[:], iota[:], idx_col[:, 1, bass.ds(i, 1)], NEVER,
                                        ALU.not_equal, ALU.mult).then_inc(pen_ready, 1)
                dve.wait_ge(pen_ready, i + 1)
                dve.wait_ge(dot_done, i + 1)
                nc.vector.scalar_tensor_tensor(out=segmax[:], in0=pen[:], scalar=logit[:, bass.ds(i, 1)],
                                               in1=segmax[:], op0=ALU.add, op1=ALU.max).then_inc(seg_done, 1)

            dve.wait_ge(consts, 13)
            make_onehot(0, 0, free=False)
            make_onehot(1, 1, free=False)
            dve.wait_ge(small_ready, 1)
            dve.wait_ge(edge_loaded, 32)
            for k in range(3):
                lo(1, 2 * k)
                lo(0, 2 * k + 1)
                table_lo(k, 0)
                lo(1, 2 * k + 1)
                lo(0, 2 * k + 2)
                table_lo(k, 1)
                for i in range(FIRST_TILE[k], min(FIRST_TILE[k + 1], 8)):
                    edge_tile(i, i % 4)
                    if i % 2 == 1:
                        make_onehot(i // 2 + 2, (i // 2) % 2)
            lo(1, 6)

            def loop_onehot(it, s):
                dve.wait_ge(batch_loaded[s], 32 * it + 128)
                dve.wait_ge(gathered, 4 * it + 2 * s + 10)
                for a in range(2):
                    for j in range(2):
                        last = nc.vector.tensor_scalar(onehot[:, s, 2 * a + j, :], idx_b[:, s, a, :],
                                                       node[:, j:j + 1], None, ALU.is_equal)
                last.then_inc(onehot_ready, 1)

            LOOPS = ET // 4 - 2
            with dve.Fori(0, LOOPS - 1) as it:
                for j in range(4):
                    edge_tile(4 * it + 8 + j, j)
                    if j % 2 == 1:
                        loop_onehot(it, j // 2)
            for i in range(ET - 4, ET):
                edge_tile(i, i % 4)

            lo(0, 7)
            lo(1, 7)
            dve.wait_ge(segall_ready, 1)

            def edge_peak(i, s):
                nc.vector.scalar_tensor_tensor(out=junk2[:, s, :], in0=iota[:], scalar=idx_col[:, 1, bass.ds(i, 1)],
                                               in1=segall[:], op0=ALU.is_equal, op1=ALU.mult,
                                               accum_out=peak[:, bass.ds(i, 1)]).then_inc(peak_done, 1)

            for s in range(2):
                edge_peak(s, s)
            with dve.Fori(1, ET // 2) as i:
                for s in range(2):
                    dve.wait_ge(peak_done, 2 * i - 1 + s)
                    edge_peak(2 * i + s, s)
            dve.wait_ge(peak_done, ET)
            link(nc.vector.tensor_scalar(peak[:], peak[:], ba_b[:, 0:1], None, ALU.add))
            link(nc.vector.tensor_scalar(logit[:], logit[:], ba_b[:, 0:1], None, ALU.add))
            nc.vector.tensor_tensor(peak[:], logit[:], peak[:], ALU.subtract).then_inc(diff_ready, 1)
            dve.wait_ge(ex_ready, 2)
            link(nc.vector.tensor_tensor(ex_lo[:], ex[:], ex_hi[:].bitcast(F32), ALU.subtract))

            def destinations(i, s):
                for part, e in enumerate((ex_hi, ex_lo)):
                    e_col = e[:, bass.ds(i, 1)]
                    last = nc.vector.tensor_scalar(oh_dst[:, s, part, :], iota[:], idx_col[:, 1, bass.ds(i, 1)],
                                                   e_col.bitcast(F32) if part == 0 else e_col,
                                                   ALU.is_equal, ALU.mult)
                last.then_inc(ohdst_ready, 1)

            lo(0, 8)
            for s in range(2):
                destinations(s, s)
            with dve.Fori(1, ET // 2) as i:
                for s in range(2):
                    dve.wait_ge(paired, 2 * i - 1 + s)
                    destinations(2 * i + s, s)
            lo(1, 8)
            dve.wait_ge(den_ready, 1)
            link(nc.vector.tensor_scalar(rden[:], bank(6)[:, 0:N], 1e-30, None, ALU.max))
            link(nc.vector.reciprocal(rden[:], rden[:]))
            for t in range(NT):
                last = nc.vector.tensor_tensor(pT[:, t, :], pT[:, t, :], rden[:], ALU.mult)
            last.then_inc(pTn_ready, 1)
            dve.wait_ge(zhi_ready, 1)
            nc.vector.tensor_tensor(zT_lo[:, :, 0:NH], high_cn[:, :, 0:NH], zT_hi[:, :, 0:NH].bitcast(F32),
                                    ALU.subtract)
            nc.vector.tensor_tensor(zT_lo[:, :, 2 * NH:PADZ], high_cn[:, :, NH:N],
                                    zT_hi[:, :, 2 * NH:PADZ].bitcast(F32), ALU.subtract).then_inc(zlo_ready, 1)
            lo(0, 9)
            lo(1, 9)
            lo(0, SLOT_W)
            dve.wait_ge(used[1], SLOT_W)
            for t in range(NT):
                last = nc.vector.scalar_tensor_tensor(out=xt[:, t, :], in0=bank(2 * t, 2), scalar=0.0,
                                                      in1=xt[:, t, :], op0=ALU.max, op1=ALU.add)
            last.then_inc(x2_ready, 1)
            dve.wait_ge(x2_ready, 1)
            layer_norm(1)
            dve.wait_ge(norm_ready, 2 * NT)
            for t in range(NT):
                last = nc.vector.tensor_tensor(xt[:, t, :], xt[:, t, :], nf[:, t, :], ALU.add)
            link(last)
            turn_lo(1)

            dve.wait_ge(h_done, 1)
            nc.vector.tensor_copy(h_sb[:], bank(0)[:, 0:NT * PD].rearrange("p (t w) -> p t w", t=NT))\
                .then_inc(h_copied, 1)
            dve.wait_ge(hT_done, 1)
            nc.vector.tensor_copy(hT_sb[:], bank(1)[0:PD, 0:N]).then_inc(hT_copied, 1)
            dve.wait_ge(sim_done, 1)
            link(nc.vector.tensor_copy(sim[:], bank(2).rearrange("p (t n) -> p t n", t=NT)))
            for t in range(NT):
                last = nc.vector.max(top[:, t, :], sim[:, t, :])
            link(last)
            for t in range(NT):
                nc.vector.tensor_scalar(tope[:, t, TOPK:2 * TOPK], top[:, t, 0:TOPK], top[:, t, 0:1], None,
                                        ALU.subtract)
                last = nc.vector.max_index(topi[:, t, :], top[:, t, :], sim[:, t, :])
            last.then_inc(top_ready, 1)
            dve.wait_ge(top_ready, 1)
            link(nc.vector.tensor_copy(topf[:], topi[:]))
            dve.wait_ge(tope_ready, NT)
            link(nc.vector.reciprocal(tsum[:, :, 1], tsum[:, :, 0]))
            for t in range(NT):
                link(nc.vector.tensor_scalar(tope[:, t, 0:TOPK], tope[:, t, 0:TOPK], tsum[:, t, 1:2], None, ALU.mult))
                link(nc.vector.tensor_scalar(route[:, t, :], iota[:], topf[:, t, 0:1], tope[:, t, 0:1],
                                             ALU.is_equal, ALU.mult))
                for k in range(1, TOPK):
                    link(nc.vector.tensor_scalar(rtmp[:, t, :], iota[:], topf[:, t, k:k + 1], tope[:, t, k:k + 1],
                                                 ALU.is_equal, ALU.mult))
                    link(nc.vector.tensor_tensor(route[:, t, :], route[:, t, :], rtmp[:, t, :], ALU.add))

            def weigh(g):
                dve.wait_ge(silu_ready, g + 1)
                for t in range(NT):
                    w = route[:, t, bass.ds(g * GX, GX)].unsqueeze(2).to_broadcast([P, GX, PD])
                    last = nc.vector.tensor_tensor(gw[:, t, :].rearrange("p (n w) -> p n w", n=GX),
                                                   act_g[:, t, :].rearrange("p (n w) -> p n w", n=GX), w, ALU.mult)
                last.then_inc(gw_ready, 1)

            def gT_lo_part(g):
                dve.wait_ge(gThi_ready, g + 1)
                nc.vector.tensor_tensor(gT_lo[:].rearrange("p b n -> p (b n)"), bank(6, 2),
                                        gT_hi[:].rearrange("p b n -> p (b n)").bitcast(F32), ALU.subtract)\
                    .then_inc(gTlo_ready, 1)

            weigh(0)
            lo(0, SLOT_W + 1)
            lo(1, SLOT_W)
            with dve.Fori(1, NG - 1) as g:
                gT_lo_part(g - 1)
                weigh(g)
                lo(0, SLOT_W + 1 + g)
                lo(1, SLOT_W + g)
            gT_lo_part(NG - 2)
            weigh(NG - 1)
            lo(1, SLOT_W + NG - 1)
            gT_lo_part(NG - 1)
            dve.wait_ge(used[1], SLOT_W + NG)
            for t in range(NT):
                nc.vector.scalar_tensor_tensor(out=xt[:, t, :], in0=bank(2 * t, 2), scalar=scale_b[:, 0:1],
                                               in1=xt[:, t, :], op0=ALU.mult, op1=ALU.add).then_inc(out_ready, 1)

        @block.tensor
        def _(pe):
            def transpose(o, i):
                k = i.shape[0]
                return nc.tensor.transpose(o, i, ident[0:k, 0:k])

            def turn(k):
                for t in range(NT):
                    pe.wait_ge(norm_ready, k * NT + t + 1)
                    for c in range(C):
                        last = transpose(high_cn[:, c, t * P:(t + 1) * P],
                                         nf[:, t, :].rearrange("p (q c) -> p c q", c=C)[:, c, :])
                last.then_inc(turned, 1)

            pe.wait_ge(consts, 13)
            turn(0)
            pe.wait_ge(idx_float, 1)
            pe.wait_ge(small_loaded, 16 * 8)
            for a in range(2):
                transpose(bank(0)[:, a * ET:(a + 1) * ET], idx_rowf[:, a, :])
            for c in range(C):
                transpose(bank(1)[:, c * PD:(c + 1) * PD], hash_w[:].rearrange("w (q c) -> w c q", c=C)[:, c, :])
            for t in range(NT):
                last = transpose(bank(2)[0:PD, t * P:(t + 1) * P], keys_n[:, t, :])
            last.then_inc(smallT, 1)
            pe.wait_ge(turned_lo, 1)
            pe.wait_ge(small_ready, 1)

            def three(o, a_hi, a_lo, b_hi, b_lo, start, stop):
                nc.tensor.matmul(o, a_hi, b_hi, start=start, stop=False)
                nc.tensor.matmul(o, a_lo, b_hi, start=False, stop=False)
                return nc.tensor.matmul(o, a_hi, b_lo, start=False, stop=stop)

            w_hi = [whi[:, s, :].rearrange("p (c n) -> p c n", c=4) for s in range(2)]
            w_lo = [wlo[:, s, :].rearrange("p (c n) -> p c n", c=4) for s in range(2)]

            def gather(i, s, q):
                for c in range(4):
                    for half in range(2):
                        for part, tab in enumerate((tab_hi, tab_lo)):
                            last = nc.tensor.matmul(bank(2 * q + half), onehot[:, s, c, (q % 2) * P:(q % 2 + 1) * P],
                                                    tab[:, c, half * HALF:(half + 1) * HALF],
                                                    start=c == 0 and part == 0, stop=c == 3 and part == 1)
                last.then_inc(gathered, 1)

            for k in range(3):
                if k:
                    pe.wait_ge(dot_done, FIRST_TILE[k])
                with pe.Fori(0, 2) as h:
                    for s in range(2):
                        pe.wait_ge(lo_ready[s], h + (2 * k + 1))
                        for cc in range(4):
                            c = 4 * s + cc
                            for t in range(NT):
                                for half in range(2):
                                    last = three(ps[:, bass.ds(h * 4 * HALF + (2 * t + half) * HALF, HALF)],
                                                 tokens(nT_hi, c, t), tokens(nT_lo, c, t),
                                                 w_hi[s][:, cc, half * HALF:(half + 1) * HALF],
                                                 w_lo[s][:, cc, half * HALF:(half + 1) * HALF],
                                                 start=c == 0, stop=c == C - 1)
                        last.then_inc(used[s], 1)
                for t in range(NT):
                    for half in range(2):
                        last = nc.tensor.matmul(bank(4 + 2 * t + half), sel[:, k, :],
                                                bias[:, half * HALF:(half + 1) * HALF], start=False, stop=True,
                                                skip_group_check=True)
                last.then_inc(biased, 1)
                for i in range(FIRST_TILE[k], min(FIRST_TILE[k + 1], 8)):
                    pe.wait_ge(tablo_ready, 2 * k + 2)
                    pe.wait_ge(onehot_ready, i // 2 + 1)
                    if i >= 4:
                        pe.wait_ge(dot_done, i - 3)
                    gather(i, (i // 2) % 2, i % 4)
            with pe.Fori(0, ET // 4 - 2) as it:
                for j in range(4):
                    pe.wait_ge(onehot_ready, 2 * it + 5 + j // 2)
                    pe.wait_ge(dot_done, 4 * it + 5 + j)
                    gather(j, j // 2, j)

            pe.wait_ge(dot_done, ET)
            sel_cols = sel[:].rearrange("q b n -> q (b n)")
            for t, first in enumerate((3 * P + NH, 4 * P)):
                for half in range(2):
                    nc.tensor.matmul(bank(2 * t + half), sel_cols[:, first:first + P],
                                     bias[:, half * HALF:(half + 1) * HALF], start=True, stop=False)

            def new_nodes(aT_hi, aT_lo, columns, u, first_kind, stop=False):
                s = u % 2
                pe.wait_ge(lo_ready[s], u // 2 + 1)
                for cc in range(4):
                    c = 4 * s + cc
                    for t in range(1 if first_kind else NT):
                        at = columns[0] if first_kind else columns[1 + t]
                        for half in range(2):
                            last = three(bank(2 * t + half), aT_hi[:, c, at:at + P], aT_lo[:, c, at:at + P],
                                         w_hi[s][:, cc, half * HALF:(half + 1) * HALF],
                                         w_lo[s][:, cc, half * HALF:(half + 1) * HALF],
                                         start=False, stop=stop and c == C - 1)
                last.then_inc(used[s], 1)
                return last

            own = (2 * NH, 0, 4 * NH)
            messages = (0, NH, 3 * NH)
            new_nodes(nT_hi, nT_lo, own, 12, True)
            new_nodes(nT_hi, nT_lo, own, 13, True)
            new_nodes(nT_hi, nT_lo, own, 14, False)
            new_nodes(nT_hi, nT_lo, own, 15, False)

            def pair(i, s, start=False, stop=False):
                pe.wait_ge(ohsrc_ready, i + 1)
                pe.wait_ge(ohdst_ready, i + 1)
                for t in range(NT):
                    for part in range(2):
                        last = nc.tensor.matmul(bank(4 + t)[:, 0:N], oh_src[:, s, t * P:(t + 1) * P],
                                                oh_dst[:, s, part, :], start=start and part == 0,
                                                stop=stop and part == 1)
                last.then_inc(paired, 1)

            pair(0, 0, start=True)
            pair(1, 1)
            with pe.Fori(1, ET // 2 - 1) as i:
                for s in range(2):
                    pair(2 * i + s, s)
            pair(ET - 2, 0)
            pair(ET - 1, 1, stop=True)
            pe.wait_ge(pT_ready, 1)
            for t in range(NT):
                last = nc.tensor.matmul(bank(6)[:, 0:N], ones[:], pT[:, t, :], start=t == 0, stop=t == NT - 1)
            last.then_inc(den_ready, 1)
            pe.wait_ge(pTn_ready, 1)
            for c in range(C):
                for t in range(NT):
                    last = nc.tensor.matmul(high_cn[:, c, :], nf[:, t, :].rearrange("p (q c) -> p c q", c=C)[:, c, :],
                                            pT[:, t, :], start=t == 0, stop=t == NT - 1)
            last.then_inc(z_ready, 1)
            pe.wait_ge(zlo_ready, 1)
            pe.wait_ge(pool_chain, 4)
            new_nodes(zT_hi, zT_lo, messages, 16, True)
            new_nodes(zT_hi, zT_lo, messages, 17, True)
            new_nodes(zT_hi, zT_lo, messages, 18, False)
            new_nodes(zT_hi, zT_lo, messages, 19, False, stop=True)

            turn(1)
            pe.wait_ge(turned_lo, 2)
            for t in range(NT):
                for c in range(C):
                    for a, aT in enumerate((nT_hi, nT_lo)):
                        for b, w in enumerate((hash_hi, hash_lo)):
                            last = nc.tensor.matmul(bank(0)[:, t * PD:(t + 1) * PD], tokens(aT, c, t), w[:, c, :],
                                                    start=c == 0 and a + b == 0, stop=c == C - 1 and a + b == 2)
            last.then_inc(h_done, 1)
            pe.wait_ge(h_copied, 1)
            for t in range(NT):
                last = transpose(bank(1)[0:PD, t * P:(t + 1) * P], h_sb[:, t, :])
            last.then_inc(hT_done, 1)
            pe.wait_ge(hT_copied, 1)
            for t in range(NT):
                last = nc.tensor.matmul(bank(2)[:, t * N:(t + 1) * N], hT_sb[:, t * P:(t + 1) * P], keysT[:],
                                        start=True, stop=True)
            last.then_inc(sim_done, 1)

            down_hi = whi[:, 0, :].rearrange("p (n c w) -> p c n w", n=GX, c=C)
            down_lo = wlo[:, 0, :].rearrange("p (n c w) -> p c n w", n=GX, c=C)

            def down(g):
                pe.wait_ge(lo_ready[0], g + (SLOT_W + 1))
                for t in range(NT):
                    for c in range(C):
                        last = three(bank(4 + t), tokens(nT_hi, c, t), tokens(nT_lo, c, t),
                                     down_hi[:, c, :, :], down_lo[:, c, :, :], start=c == 0, stop=c == C - 1)
                last.then_inc(used[0], 1)

            def turn_group(g):
                pe.wait_ge(gw_ready, g + 1)
                for b in range(BLOCKS):
                    for t in range(NT):
                        last = transpose(ps[:, 6 * HALF + b * N + t * P:6 * HALF + b * N + (t + 1) * P],
                                         gw[:, t, b * P:(b + 1) * P])
                last.then_inc(gT_done, 1)

            def up(g, stop=False):
                pe.wait_ge(lo_ready[1], g + (SLOT_W + 1))
                pe.wait_ge(gTlo_ready, g + 1)
                for b in range(BLOCKS):
                    for t in range(NT):
                        for half in range(2):
                            last = three(bank(2 * t + half), gT_hi[:, b, t * P:(t + 1) * P],
                                         gT_lo[:, b, t * P:(t + 1) * P],
                                         w_hi[1][:, b, half * HALF:(half + 1) * HALF],
                                         w_lo[1][:, b, half * HALF:(half + 1) * HALF],
                                         start=False, stop=stop and b == BLOCKS - 1)
                last.then_inc(used[1], 1)

            down(0)
            turn_group(0)
            for b in range(4):
                nc.tensor.matmul(bank(b), sel[0:1, 1, :], sel_cols[0:1, P:P + HALF], start=True, stop=False)
            with pe.Fori(1, NG) as g:
                pe.wait_ge(silu_ready, g)
                down(g)
                up(g - 1)
                turn_group(g)
            up(NG - 1, stop=True)



_INS = ['x', 'src', 'dst', 'L0_gnn_W_hh', 'L0_gnn_b_hh', 'L0_gnn_W_oo', 'L0_gnn_b_oo', 'L0_gnn_W_ho', 'L0_gnn_b_ho',
        'L0_gnn_W_a', 'L0_gnn_b_a', 'L0_gnn_W_hn', 'L0_gnn_b_hn', 'L0_gnn_W_on', 'L0_gnn_b_on', 'L0_ffn_hasher_w',
        'L0_ffn_keys', 'L0_ffn_values_down', 'L0_ffn_values_up', 'L0_ffn_scale']


def kernel(**inputs):
    import numpy as _np
    import concourse.bacc as _bacc
    from concourse import mybir as _mybir
    from concourse.bass_utils import run_bass_kernel_spmd as _run

    nc = _bacc.Bacc("TRN2", target_bir_lowering=False, num_devices=1)
    arrays, args = {}, []
    for name in _INS:
        a = _np.ascontiguousarray(inputs[name])
        arrays[f"in_{name}_dram"] = a
        args.append(nc.dram_tensor(f"in_{name}_dram", a.shape, _mybir.dt.from_np(a.dtype), kind="ExternalInput").ap())
    out = nc.dram_tensor("out_0_dram", (N, D), _mybir.dt.float32, kind="ExternalOutput").ap()
    gnn_ffn(nc, *args, out)
    r = _run(nc, [arrays], core_ids=[0])
    return r.results[0]["out_0_dram"]
```

```python
from contextlib import ExitStack

import concourse.bass as bass
from concourse import mybir
from concourse.alu_op_type import AluOpType as ALU

F32 = mybir.dt.float32
F32R = mybir.dt.float32r
BF16 = mybir.dt.bfloat16
F16 = mybir.dt.float16
I32 = mybir.dt.int32
U32 = mybir.dt.uint32
ACT = mybir.ActivationFunctionType
RMAX = bass.bass_isa.ReduceOp.max

P = 128
N = 256
NT = N // P
D = 1024
C = D // P
HALF = 512
NH = 64
PADN = N + 2 * NH
PADZ = N + NH
E = 8192
ET = E // P
FIRST_TILE = [0, 1, 6, ET]
BATCH = 2 * P
NB = E // BATCH
GROUP = 4
EG = ET // GROUP
OB = 8
HEAD_START = 4
POOL_TILES = 40
ACT_TILES = ET - POOL_TILES
ACT_HEAD = 8
XP = 256
PD = 32
TOPK = 4
GX = 16
NG = XP // GX
UNIT = 4096
WUNITS = 20
POOL_UNITS = [(0, 7), (1, 7)]
SLOT_W = WUNITS // 2
LAST = SLOT_W + NG
EPS = 1e-5
NEVER = -3.0e38
BLOCKS = GX * PD // P


def gnn_ffn(nc, x, src, dst, W_hh, b_hh, W_oo, b_oo, W_ho, b_ho, W_a, b_a, W_hn, b_hn, W_on, b_on,
            hasher_w, keys, values_down, values_up, scale, out):
    ctx = ExitStack()
    with ctx:
        def sb(name, shape, dt=F32, where=ctx):
            return where.enter_context(nc.sbuf_tensor(name, shape, dt))

        def sem(name):
            return ctx.enter_context(nc.semaphore(name))

        raw = sb("raw", [P, 2, UNIT])
        whi = sb("whi", [P, 2, UNIT], F32R)
        wlo = sb("wlo", [P, 2, UNIT], F32R)
        xt = sb("xt", [P, NT, D])
        wa_b = xt[:, 1, :]
        nf = sb("nf", [P, NT, D])
        nT_hi = sb("nT_hi", [P, C, PADN], F32R)
        nT_lo = sb("nT_lo", [P, C, PADN], F32R)
        iota = sb("iota", [P, N])
        iota16 = sb("iota16", [P, N], F16)
        node = sb("node", [P, 2])
        row_no = sb("row_no", [P, 1])
        ident = sb("ident", [P, P])
        sel = sb("sel", [5, 5, P], F32R)
        sel_ones = sb("sel_ones", [5, 1])
        bias_hi = sb("bias_hi", [5, D], F32R)
        bias_lo = sb("bias_lo", [5, D], F32R)
        segmax = sb("segmax", [P, N])
        segall = sb("segall", [P, N])
        logit = sb("logit", [P, ET])
        peak = sb("peak", [P, ET])
        ex = sb("ex", [P, ET])
        ex_16 = sb("ex_16", [P, ET], F16)
        ex_hi = sb("ex_hi", [P, ET])
        ex_lo = sb("ex_lo", [P, ET])
        src_neg = sb("src_neg", [P, ET])
        idx_col = sb("idx_col", [P, 2, ET])
        scale_b = sb("scale_b", [P, 1])
        ba_b = sb("ba_b", [P, 1])
        stats = sb("stats", [P, NT, 2, 6])
        mv = sb("mv", [P, NT, 2])
        ln = sb("ln", [P, 5, NT])
        with ExitStack() as early:
            idx_rows = sb("idx_rows", [ET, 2, P], I32, early)
            idx_rowf = sb("idx_rowf", [ET, 2, P], F32, early)
            group_ends = sb("group_ends", [EG, 5], F32, early)
            bias = sb("bias", [5, D], F32, early)
        halves = sb("halves", [1, EG], I32)
        with ExitStack() as edge:
            tab_hi = sb("tab_hi", [P, 4, D], F32R, edge)
            tab_lo = sb("tab_lo", [P, 4, D], F32R, edge)
            onehot = sb("onehot", [P, 2, 4, BATCH], F32R, edge)
            idx_b = sb("idx_b", [P, 2, 2, BATCH], I32, edge)
            junk = sb("junk", [P, D], BF16, edge)
            pen = sb("pen", [P, N], F32, edge)
        group_rows = junk[0:EG, :].bitcast(I32)
        feat_hi = tab_hi[:, 2:4, :].rearrange("p a (c e) -> p (a c) e", e=P)
        feat_lo = tab_lo[:, 2:4, :].rearrange("p a (c e) -> p (a c) e", e=P)
        ones = sb("ones", [P, P])
        hash_w = sb("hash_w", [PD, D])
        hashT = sb("hashT", [P, C, PD])
        keys_n = sb("keys_n", [P, NT, PD])
        keysT = sb("keysT", [PD, XP])
        with ExitStack() as late:
            pT = sb("pT", [P, NT, N], F32, late)
            rden = sb("rden", [P, N], F32, late)
            with ExitStack() as pairs:
                junk2 = sb("junk2", [P, 4, N], BF16, pairs)
                distance = sb("distance", [P, 4, N], F16, pairs)
                oh_src = sb("oh_src", [P, ET, N], F16, pairs)
                oh_dst = sb("oh_dst", [P, OB, 2, N], F16, pairs)
            zT_hi = sb("zT_hi", [P, C, PADZ], F32R, late)
            zT_lo = sb("zT_lo", [P, C, PADZ], F32R, late)
        hT_sb = sb("hT_sb", [PD, N])
        sim = sb("sim", [P, NT, XP])
        top = sb("top", [P, NT, 8])
        topi = sb("topi", [P, NT, 8], U32)
        topf = sb("topf", [P, NT, 8])
        tope = sb("tope", [P, NT, 8])
        tsum = sb("tsum", [P, NT, 2])
        route = sb("route", [P, NT, XP])
        rtmp = sb("rtmp", [P, 2, XP])
        act_g = sb("act_g", [P, NT, GX * PD])
        gw = sb("gw", [P, NT, GX * PD])
        gT_hi = sb("gT_hi", [P, BLOCKS, N], F32R)
        gT_lo = sb("gT_lo", [P, BLOCKS, N], F32R)

        ps = ctx.enter_context(nc.psum_tensor("ps", [P, 8 * HALF], F32))

        def bank(b, n=1):
            return ps[:, b * HALF:(b + n) * HALF]

        turned_cn = [[bank(4 * k + 2 * t, 2).rearrange("p (c n) -> p c n", c=C) for t in range(NT)]
                     for k in range(2)]
        high_cn = bank(4, 4).rearrange("p (c n) -> p c n", c=C)

        x_loaded = [sem(f"x_loaded{t}") for t in range(NT)]
        idx_loaded = sem("idx_loaded")
        small_loaded = sem("small_loaded")
        edge_loaded = sem("edge_loaded")
        batch_loaded = [sem(f"batch_loaded{s}") for s in range(2)]
        loaded = [sem(f"loaded{s}") for s in range(2)]
        hi_ready = [sem(f"hi_ready{s}") for s in range(2)]
        lo_ready = [sem(f"lo_ready{s}") for s in range(2)]
        used = [sem(f"used{s}") for s in range(2)]
        consts = sem("consts")
        pool_chain = sem("pool_chain")
        chain = sem("chain")
        var_ready = sem("var_ready")
        root_ready = sem("root_ready")
        norm_ready = sem("norm_ready")
        turned = sem("turned")
        turned_hi = sem("turned_hi")
        turned_lo = sem("turned_lo")
        picker_ready = sem("picker_ready")
        feat_done = sem("feat_done")
        feathi_ready = sem("feathi_ready")
        featlo_ready = sem("featlo_ready")
        idx_float = sem("idx_float")
        group_loaded = sem("group_loaded")
        smallT = sem("smallT")
        small_ready = sem("small_ready")
        table_done = sem("table_done")
        tabhi_ready = sem("tabhi_ready")
        tablo_ready = sem("tablo_ready")
        onehot_ready = sem("onehot_ready")
        gathered = sem("gathered")
        pen_ready = sem("pen_ready")
        dot_done = sem("dot_done")
        seg_done = sem("seg_done")
        segall_ready = sem("segall_ready")
        peak_done = sem("peak_done")
        diff_ready = sem("diff_ready")
        ex_ready = sem("ex_ready")
        exlo_ready = sem("exlo_ready")
        src_pool = sem("src_pool")
        distance_ready = sem("distance_ready")
        src_act = sem("src_act")
        oh_ready = sem("oh_ready")
        z_zeroed = sem("z_zeroed")
        bias_ready = sem("bias_ready")
        x_again = sem("x_again")
        hash_loaded = sem("hash_loaded")
        hash_turned = sem("hash_turned")
        hash_ready = sem("hash_ready")
        paired = sem("paired")
        pT_ready = sem("pT_ready")
        den_ready = sem("den_ready")
        pTn_ready = sem("pTn_ready")
        z_ready = sem("z_ready")
        zhi_ready = sem("zhi_ready")
        zlo_ready = sem("zlo_ready")
        nodes_done = sem("nodes_done")
        x2_ready = sem("x2_ready")
        hT_done = sem("hT_done")
        hT_copied = sem("hT_copied")
        sim_done = sem("sim_done")
        top_ready = sem("top_ready")
        tope_ready = sem("tope_ready")
        silu_ready = sem("silu_ready")
        gw_ready = sem("gw_ready")
        gT_done = sem("gT_done")
        gThi_ready = sem("gThi_ready")
        gTlo_ready = sem("gTlo_ready")
        summed = sem("summed")
        out_ready = sem("out_ready")
        stored = sem("stored")

        def pair_of(i):
            return (i - FIRST_TILE[1 if i < FIRST_TILE[2] else 2]) % 4

        def rows(w, half, quarter):
            v = w[half * D:(half + 1) * D, :].rearrange("(p c) n -> p c n", c=C)
            return v[:, 4 * quarter:4 * quarter + 4, :]

        unit_source = [rows(w, h, q) for w in (W_hh, W_oo, W_ho) for h in range(2) for q in range(2)]
        unit_source += [rows(w, h, q) for h in range(2) for w in (W_hn, W_on) for q in range(2)]
        down_v = values_down.rearrange("n (p c) w -> p n (c w)", c=C)
        up_v = values_up.rearrange("n w d -> (n w) d").rearrange("(b q) d -> q b d", q=P)
        raw_down = raw[:, 0, :].rearrange("p (n k) -> p n k", n=GX)
        raw_up = [raw[:, s, :].rearrange("p (b d) -> p b d", b=BLOCKS) for s in range(2)]

        def half(t, s, j, down=False):
            if down:
                return t[:, s, :].rearrange("p (n k) -> p n k", n=GX)[:, :, j * 4 * PD:(j + 1) * 4 * PD]
            return t[:, s, j * UNIT // 2:(j + 1) * UNIT // 2]

        def tokens(t3, c, t):
            return t3[:, c, NH:NH + P] if t == 0 else t3[:, c, 4 * NH:PADN]

        def token_columns(k, t):
            if t == 1:
                return ((4 * NH, 0, P),)
            return ((NH, NH, NH), (2 * NH, 0, NH)) if k == 0 else ((2 * NH, 0, P),)

        block = ctx.enter_context(nc.Block())

        @block.sync
        def _(sp):
            x_v = x.rearrange("(t p) n -> p t n", p=P)
            for t in range(NT):
                sp.dma_start(xt[:, t, :], x_v[:, t, :]).then_inc(x_loaded[t], 16)
            for u in range(WUNITS):
                s, n = u % 2, u // 2
                if n:
                    sp.wait_ge(lo_ready[s], 2 * n)
                if u == 16:
                    sp.wait_ge(seg_done, ET)
                    sp.dma_start(xt[:, 1, :], x_v[:, 1, :]).then_inc(x_again, 16)
                    sp.dma_start(hash_w[:], hasher_w).then_inc(hash_loaded, 16)
                    sp.dma_start(keys_n[:], keys.rearrange("(t p) w -> p t w", p=P)).then_inc(hash_loaded, 16)
                dst_ap = raw[:, s, :].rearrange("p (c n) -> p c n", c=4)
                sp.dma_start(dst_ap, unit_source[u]).then_inc(loaded[s], 16)
            sp.wait_ge(lo_ready[0], 2 * SLOT_W)
            sp.dma_start(raw_down, down_v[:, 0:GX, :]).then_inc(loaded[0], 16)
            with sp.Fori(0, NG - 1) as g:
                sp.wait_ge(lo_ready[0], 2 * g + 2 * (SLOT_W + 1))
                sp.dma_start(raw_down, down_v[:, bass.ds((g + 1) * GX, GX), :]).then_inc(loaded[0], 16)
                sp.wait_ge(lo_ready[1], 2 * g + 2 * SLOT_W)
                sp.dma_start(raw_up[1], up_v[:, bass.ds(g * BLOCKS, BLOCKS), :]).then_inc(loaded[1], 16)
            sp.wait_ge(lo_ready[0], 2 * LAST)
            sp.dma_start(raw_up[0], up_v[:, (NG - 1) * BLOCKS:NG * BLOCKS, :]).then_inc(loaded[0], 16)
            out_v = out.rearrange("(t p) n -> p t n", p=P)
            for t in range(NT):
                sp.wait_ge(out_ready, t + 1)
                sp.dma_start(out_v[:, t, :], xt[:, t, :]).then_inc(stored, 16)
            sp.wait_ge(stored, 16 * NT)

        @block.gpsimd
        def _(pool):
            def load_batch(b, s):
                pool.dma_start(idx_b[:, s, 0, :], src[bass.ds(b * BATCH, BATCH)].partition_broadcast(P))\
                    .then_inc(batch_loaded[s], 16)
                pool.dma_start(idx_b[:, s, 1, :], dst[bass.ds(b * BATCH, BATCH)].partition_broadcast(P))\
                    .then_inc(batch_loaded[s], 16)

            load_batch(0, 0)
            load_batch(1, 1)
            made = [0]

            def constant(ins):
                made[0] += 1
                ins.then_inc(consts, 1)
                pool.wait_ge(consts, made[0])

            nc.gpsimd.memset(ident[:], 0.0).then_inc(pool_chain, 1)
            nc.gpsimd.memset(sel_ones[:], 1.0).then_inc(pool_chain, 1)
            pool.wait_ge(pool_chain, 2)
            constant(nc.gpsimd.affine_select(out=ident[:], in_=ident[:], compare_op=ALU.not_equal, fill=1.0,
                                             base=0, pattern=[[-1, P]], channel_multiplier=1))
            constant(nc.gpsimd.affine_select(out=sel[:], in_=sel_ones[:].unsqueeze(2).to_broadcast([5, 5, P]), compare_op=ALU.is_equal, fill=0.0,
                                             base=0, pattern=[[-1, 5], [0, P]], channel_multiplier=1))
            for T in (nT_hi, nT_lo):
                for at in (0, 3 * NH):
                    constant(nc.gpsimd.memset(T[:, :, at:at + NH].bitcast(F32), 0.0))
            for col, part, base in ((0, 0, NH), (0, NH, 0), (1, 0, P), (1, NH, P + NH)):
                constant(nc.gpsimd.iota(node[part:part + NH, col:col + 1], pattern=[[0, 1]], base=base,
                                        channel_multiplier=1, allow_small_or_imprecise_dtypes=True))
            constant(nc.gpsimd.iota(row_no[:], pattern=[[0, 1]], base=0, channel_multiplier=1,
                                    allow_small_or_imprecise_dtypes=True))
            constant(nc.gpsimd.iota(iota[:], pattern=[[1, N]], base=0, channel_multiplier=0,
                                    allow_small_or_imprecise_dtypes=True))
            constant(nc.gpsimd.tensor_copy(iota16[:], iota[:]))
            constant(nc.gpsimd.memset(segmax[:], NEVER))

            with pool.Fori(1, NB // 2) as i:
                for s in range(2):
                    pool.wait_ge(onehot_ready, 2 * i - 1 + s)
                    load_batch(2 * i + s, s)

            pool.wait_ge(seg_done, ET)
            nc.gpsimd.partition_all_reduce(segall[:], segmax[:], P, RMAX).then_inc(segall_ready, 1)

            def pool_lo(s, n):
                for j in range(2):
                    pool.wait_ge(hi_ready[s], 2 * n + j + 1)
                    nc.gpsimd.tensor_tensor(half(wlo, s, j), half(raw, s, j), half(whi, s, j).bitcast(F32),
                                            ALU.subtract).then_inc(lo_ready[s], 1)

            for i in range(POOL_TILES):
                if i == HEAD_START:
                    pool_lo(*POOL_UNITS[0])
                nc.gpsimd.tensor_scalar(oh_src[:, ACT_TILES + i, :], iota16[:],
                                        idx_col[:, 0, ACT_TILES + i:ACT_TILES + i + 1], None,
                                        ALU.is_equal).then_inc(src_pool, 1)
            pool_lo(*POOL_UNITS[1])
            nc.gpsimd.memset(ones[:], 1.0).then_inc(pool_chain, 1)
            pool.wait_ge(paired, ET)
            nc.gpsimd.memset(zT_hi[:, :, NH:2 * NH].bitcast(F32), 0.0).then_inc(z_zeroed, 1)
            nc.gpsimd.memset(zT_lo[:, :, NH:2 * NH].bitcast(F32), 0.0).then_inc(z_zeroed, 1)

        @block.scalar
        def _(act):
            act.dma_start(group_rows, dst.rearrange("(g n) -> g n", g=EG)).then_inc(group_loaded, 16)
            act.dma_start(idx_rows[:, 0, :], src.rearrange("(t p) -> t p", p=P)).then_inc(idx_loaded, 16)
            act.dma_start(idx_rows[:, 1, :], dst.rearrange("(t p) -> t p", p=P)).then_inc(idx_loaded, 16)
            for q, b in enumerate((b_hh, b_oo, b_ho, b_hn, b_on)):
                act.dma_start(bias[q:q + 1, :], b.rearrange("(a n) -> a n", a=1)).then_inc(small_loaded, 16)
            act.dma_start(scale_b[:], scale.partition_broadcast(P)).then_inc(small_loaded, 16)
            act.dma_start(ba_b[:], b_a.partition_broadcast(P)).then_inc(edge_loaded, 16)

            def root(k):
                for t in range(NT):
                    act.wait_ge(var_ready, NT * k + t + 1)
                    nc.scalar.activation(ln[:, 1, t:t + 1], ln[:, 0, t:t + 1], ACT.Sqrt).then_inc(root_ready, 1)

            def turn_hi(k):
                for t in range(NT):
                    act.wait_ge(turned, NT * k + t + 1)
                    for to, at, w in token_columns(k, t):
                        last = nc.scalar.activation(nT_hi[:, :, to:to + w], turned_cn[k][t][:, :, at:at + w], ACT.Copy)
                    last.then_inc(turned_hi, 1)

            def hi(s, n, first=False, down=False, other=False):
                act.wait_ge(loaded[s], 16 * n + 16)
                for j in range(2):
                    if not first:
                        act.wait_ge(used[s], 2 * n + (0 if other else j - 1))
                    nc.scalar.activation(half(whi, s, j, down), half(raw, s, j, down), ACT.Copy)\
                        .then_inc(hi_ready[s], 1)

            root(0)
            act.wait_ge(norm_ready, NT)
            act.dma_start(wa_b, W_a.rearrange("n a -> (n a)").partition_broadcast(P)).then_inc(edge_loaded, 16)
            hi(0, 0, first=True)
            act.wait_ge(small_loaded, 16 * 6)
            nc.scalar.activation(bias_hi[:], bias[:], ACT.Copy).then_inc(bias_ready, 1)
            for h in range(2):
                act.wait_ge(feat_done, h + 1)
                nc.scalar.activation(feat_hi[:, C * h:C * h + C, :].rearrange("p c e -> p (c e)"),
                                     bank(4 + 2 * h, 2), ACT.Copy).then_inc(feathi_ready, 1)
            hi(1, 0, first=True)
            turn_hi(0)
            hi(0, 1)
            hi(1, 1)
            hi(0, 2)
            def table_hi(k, h):
                for t in range(NT):
                    if t == 0:
                        act.wait_ge(table_done, 2 * (k - 1) + h + 1)
                    else:
                        act.wait_ge(used[1], 4 * k + 2 * h + 2)
                    act.wait_ge(gathered, FIRST_TILE[k])
                    nc.scalar.activation(tab_hi[:, 2 * h + t, :], bank(4 * h + 2 * t, 2), ACT.Copy)\
                        .then_inc(tabhi_ready, 1)

            for k in (1, 2):
                hi(1, 2 * k)
                hi(0, 2 * k + 1)
                table_hi(k, 0)
                hi(1, 2 * k + 1)
                hi(0, 2 * k + 2)
                table_hi(k, 1)
            hi(1, 6)

            def source_rows(m):
                for pair in ((0, 1), (2, 3)):
                    for s in pair:
                        nc.scalar.activation(distance[:, s, :], iota16[:], ACT.Abs,
                                             bias=src_neg[:, bass.ds(4 * m + s, 1)]).then_inc(distance_ready, 1)
                    for s in pair:
                        act.wait_ge(distance_ready, 4 * m + s + 1)
                        nc.scalar.activation(oh_src[:, bass.ds(4 * m + s, 1), :].rearrange("p a n -> p (a n)"),
                                             distance[:, s, :], ACT.Relu, bias=1.0, scale=-1.0)\
                            .then_inc(src_act, 1)

            act.wait_ge(seg_done, ET)
            with act.Fori(0, ACT_HEAD // 4) as m:
                source_rows(m)
            hi(0, 7)
            hi(1, 7)
            with act.Fori(ACT_HEAD // 4, ACT_TILES // 4) as m:
                source_rows(m)
            act.wait_ge(diff_ready, 1)
            nc.scalar.activation(ex[:], peak[:], ACT.Exp).then_inc(ex_ready, 1)
            act.wait_ge(ex_ready, 1)
            nc.scalar.activation(ex_16[:], ex[:], ACT.Copy).then_inc(ex_ready, 1)

            hi(0, 8)
            act.wait_ge(paired, ET)
            nc.scalar.activation(pT[:], bank(4, 2).rearrange("p (t n) -> p t n", t=NT)[:, :, 0:N], ACT.Copy)\
                .then_inc(pT_ready, 1)
            act.wait_ge(z_ready, 1)
            nc.scalar.activation(zT_hi[:, :, 0:NH], high_cn[:, :, 0:NH], ACT.Copy)
            nc.scalar.activation(zT_hi[:, :, 2 * NH:PADZ], high_cn[:, :, NH:N], ACT.Copy).then_inc(zhi_ready, 1)
            hi(1, 8)
            hi(0, 9)
            hi(1, 9)
            hi(0, SLOT_W, down=True, other=True)
            root(1)
            turn_hi(1)
            act.wait_ge(top_ready, 1)
            for t in range(NT):
                nc.scalar.activation(tope[:, t, 0:TOPK], tope[:, t, TOPK:2 * TOPK], ACT.Exp,
                                     accum_out=tsum[:, t, 0:1]).then_inc(tope_ready, 1)

            d_cols = bank(4, 2)
            t_cols = bank(6, 2)

            def silu(g):
                act.wait_ge(used[0], 2 * g + 2 * (SLOT_W + 1))
                nc.scalar.activation(act_g[:].rearrange("p t n -> p (t n)"), d_cols, ACT.Silu)\
                    .then_inc(silu_ready, 1)

            def gT_hi_part(g):
                act.wait_ge(gT_done, g + 1)
                nc.scalar.activation(gT_hi[:].rearrange("p b n -> p (b n)"), t_cols, ACT.Copy)\
                    .then_inc(gThi_ready, 1)

            silu(0)
            hi(0, SLOT_W + 1, down=True)
            hi(1, SLOT_W)
            with act.Fori(1, NG - 1) as g:
                gT_hi_part(g - 1)
                silu(g)
                hi(0, g + (SLOT_W + 1), down=True)
                hi(1, g + SLOT_W)
            gT_hi_part(NG - 2)
            silu(NG - 1)
            hi(0, LAST, other=True)
            gT_hi_part(NG - 1)

        @block.vector
        def _(dve):
            links = [0]

            def link(ins):
                links[0] += 1
                ins.then_inc(chain, 1)
                dve.wait_ge(chain, links[0])

            def lo(s, n, down=False):
                for j in range(2):
                    dve.wait_ge(hi_ready[s], 2 * n + (j + 1))
                    nc.vector.tensor_tensor(half(wlo, s, j, down), half(raw, s, j, down),
                                            half(whi, s, j, down).bitcast(F32), ALU.subtract)\
                        .then_inc(lo_ready[s], 1)

            def layer_norm(k, t):
                for j in range(2):
                    last = nc.vector.bn_stats(stats[:, t, j, :], xt[:, t, j * HALF:(j + 1) * HALF])
                link(last)
                link(nc.vector.bn_aggr(mv[:, t, :], stats[:, t, :, :].rearrange("p j s -> p (j s)")))
                var, root, inverse, other, rstd = (ln[:, q, t:t + 1] for q in range(5))
                nc.vector.tensor_scalar(var, mv[:, t, 1:2], EPS, None, ALU.add).then_inc(var_ready, 1)
                dve.wait_ge(root_ready, NT * k + t + 1)
                link(nc.vector.reciprocal(inverse, root))
                link(nc.vector.scalar_tensor_tensor(out=other, in0=inverse, scalar=var, in1=root,
                                                    op0=ALU.mult, op1=ALU.add))
                link(nc.vector.tensor_scalar(inverse, other, 0.5, None, ALU.mult))
                link(nc.vector.reciprocal(rstd, inverse))
                nc.vector.tensor_scalar(nf[:, t, :], xt[:, t, :], mv[:, t, 0:1], rstd,
                                        ALU.subtract, ALU.mult).then_inc(norm_ready, 1)

            def turn_lo(k):
                for t in range(NT):
                    dve.wait_ge(turned_hi, NT * k + t + 1)
                    for to, at, w in token_columns(k, t):
                        last = nc.vector.tensor_tensor(nT_lo[:, :, to:to + w], turned_cn[k][t][:, :, at:at + w],
                                                       nT_hi[:, :, to:to + w].bitcast(F32), ALU.subtract)
                    last.then_inc(turned_lo, 1)

            for t in range(NT):
                dve.wait_ge(x_loaded[t], 16)
                layer_norm(0, t)
            dve.wait_ge(consts, 14)
            dve.wait_ge(batch_loaded[0], 32)
            for a in range(2):
                for j, number in enumerate((row_no[:, 0:1], node[:, 1:2])):
                    last = nc.vector.tensor_scalar(onehot[:, 1, 2 * a + j, 0:P], idx_b[:, 0, a, 0:P], number, None,
                                                   ALU.is_equal)
            last.then_inc(picker_ready, 1)
            dve.wait_ge(group_loaded, 16)
            nc.vector.tensor_reduce(group_ends[:, 0:1], group_rows, mybir.AxisListType.X, ALU.min)
            link(nc.vector.tensor_reduce(group_ends[:, 1:2], group_rows, mybir.AxisListType.X, ALU.max))
            nc.vector.tensor_scalar(group_ends[:, 2:3], group_ends[:, 0:1], float(P), None, ALU.is_lt)
            link(nc.vector.tensor_scalar(group_ends[:, 3:4], group_ends[:, 1:2], float(P), 2.0, ALU.is_ge, ALU.mult))
            nc.vector.tensor_tensor(group_ends[:, 4:5], group_ends[:, 2:3], group_ends[:, 3:4], ALU.add)
            dve.wait_ge(idx_loaded, 32)
            nc.vector.tensor_copy(idx_rowf[:], idx_rows[:]).then_inc(idx_float, 1)
            lo(0, 0)
            dve.wait_ge(bias_ready, 1)
            nc.vector.tensor_tensor(bias_lo[:], bias[:], bias_hi[:].bitcast(F32), ALU.subtract).then_inc(bias_ready, 1)
            for h in range(2):
                dve.wait_ge(feathi_ready, h + 1)
                both = slice(C * h, C * h + C)
                nc.vector.tensor_tensor(feat_lo[:, both, :].rearrange("p c e -> p (c e)"), bank(4 + 2 * h, 2),
                                        feat_hi[:, both, :].rearrange("p c e -> p (c e)").bitcast(F32),
                                        ALU.subtract).then_inc(featlo_ready, 1)
            lo(1, 0)
            turn_lo(0)
            dve.wait_ge(smallT, 1)
            nc.vector.tensor_copy(idx_col[:].rearrange("p a t -> p (a t)"), bank(4)[:, 0:2 * ET])
            nc.vector.tensor_scalar(src_neg[:], bank(4)[:, 0:ET], -1.0, None, ALU.mult)
            nc.vector.tensor_copy(halves[:], bank(5)[0:1, 0:EG]).then_inc(small_ready, 1)
            lo(0, 1)
            lo(1, 1)
            lo(0, 2)

            def table_lo(k, h):
                for t in range(NT):
                    dve.wait_ge(tabhi_ready, 4 * (k - 1) + 2 * h + t + 1)
                    nc.vector.tensor_tensor(tab_lo[:, 2 * h + t, :], bank(4 * h + 2 * t, 2),
                                            tab_hi[:, 2 * h + t, :].bitcast(F32), ALU.subtract)\
                        .then_inc(tablo_ready, 1)

            def make_onehot(b, s, free=True):
                dve.wait_ge(batch_loaded[s], 32 * (b // 2 + 1))
                if free:
                    dve.wait_ge(gathered, 2 * b - 2)
                for a in range(2):
                    for j in range(2):
                        last = nc.vector.tensor_scalar(onehot[:, s, 2 * a + j, :], idx_b[:, s, a, :],
                                                       node[:, j:j + 1], None, ALU.is_equal)
                last.then_inc(onehot_ready, 1)

            def edge_tile(i, q):
                dve.wait_ge(gathered, i + 1)
                nc.vector.scalar_tensor_tensor(out=junk[:], in0=bank(2 * q, 2), scalar=0.0, in1=wa_b[:],
                                               op0=ALU.max, op1=ALU.mult,
                                               accum_out=logit[:, bass.ds(i, 1)]).then_inc(dot_done, 1)
                if not isinstance(i, int) or i:
                    dve.wait_ge(seg_done, i)
                nc.vector.tensor_scalar(pen[:], iota[:], idx_col[:, 1, bass.ds(i, 1)], NEVER,
                                        ALU.not_equal, ALU.mult).then_inc(pen_ready, 1)
                dve.wait_ge(pen_ready, i + 1)
                dve.wait_ge(dot_done, i + 1)
                nc.vector.scalar_tensor_tensor(out=segmax[:], in0=pen[:], scalar=logit[:, bass.ds(i, 1)],
                                               in1=segmax[:], op0=ALU.add, op1=ALU.max).then_inc(seg_done, 1)

            make_onehot(0, 0, free=False)
            dve.wait_ge(feat_done, 2)
            make_onehot(1, 1, free=False)
            dve.wait_ge(small_ready, 1)
            dve.wait_ge(edge_loaded, 32)
            edge_tile(0, pair_of(0))
            for k in (1, 2):
                lo(1, 2 * k)
                lo(0, 2 * k + 1)
                table_lo(k, 0)
                lo(1, 2 * k + 1)
                lo(0, 2 * k + 2)
                table_lo(k, 1)
                for i in range(FIRST_TILE[k], min(FIRST_TILE[k + 1], 8)):
                    edge_tile(i, pair_of(i))
                    if i % 2 == 1:
                        make_onehot(i // 2 + 2, (i // 2) % 2)
            lo(1, 6)

            def loop_onehot(it, s):
                dve.wait_ge(batch_loaded[s], 32 * it + 128)
                dve.wait_ge(gathered, 4 * it + 2 * s + 10)
                for a in range(2):
                    for j in range(2):
                        last = nc.vector.tensor_scalar(onehot[:, s, 2 * a + j, :], idx_b[:, s, a, :],
                                                       node[:, j:j + 1], None, ALU.is_equal)
                last.then_inc(onehot_ready, 1)

            LOOPS = ET // 4 - 2
            with dve.Fori(0, LOOPS - 1) as it:
                for j in range(4):
                    edge_tile(4 * it + 8 + j, pair_of(8 + j))
                    if j % 2 == 1:
                        loop_onehot(it, j // 2)
            for i in range(ET - 4, ET):
                edge_tile(i, pair_of(i))
            dve.wait_ge(segall_ready, 1)

            def edge_peak(i, s):
                nc.vector.scalar_tensor_tensor(out=junk2[:, s, :], in0=iota[:], scalar=idx_col[:, 1, bass.ds(i, 1)],
                                               in1=segall[:], op0=ALU.is_equal, op1=ALU.mult,
                                               accum_out=peak[:, bass.ds(i, 1)]).then_inc(peak_done, 1)

            for s in range(4):
                edge_peak(s, s)
            with dve.Fori(1, ET // 4) as i:
                for s in range(4):
                    dve.wait_ge(peak_done, 4 * i - 3 + s)
                    edge_peak(4 * i + s, s)
            dve.wait_ge(peak_done, ET)
            link(nc.vector.tensor_scalar(peak[:], peak[:], ba_b[:, 0:1], None, ALU.add))
            link(nc.vector.tensor_scalar(logit[:], logit[:], ba_b[:, 0:1], None, ALU.add))
            nc.vector.tensor_tensor(peak[:], logit[:], peak[:], ALU.subtract).then_inc(diff_ready, 1)
            dve.wait_ge(ex_ready, 2)
            link(nc.vector.tensor_copy(ex_hi[:], ex_16[:]))
            link(nc.vector.tensor_tensor(ex_lo[:], ex[:], ex_hi[:], ALU.subtract))

            def onehot_rows(i, s):
                for part, e in enumerate((ex_hi, ex_lo)):
                    last = nc.vector.tensor_scalar(oh_dst[:, s, part, :], iota16[:], idx_col[:, 1, bass.ds(i, 1)],
                                                   e[:, bass.ds(i, 1)], ALU.is_equal, ALU.mult)
                last.then_inc(oh_ready, 1)

            for s in range(OB):
                onehot_rows(s, s)
            with dve.Fori(1, ET // OB) as i:
                for s in range(OB):
                    dve.wait_ge(paired, OB * i + (s - OB + 1))
                    onehot_rows(OB * i + s, s)
            dve.wait_ge(den_ready, 1)
            link(nc.vector.tensor_scalar(rden[:], bank(6)[:, 0:N], 1e-30, None, ALU.max))
            link(nc.vector.reciprocal(rden[:], rden[:]))
            for t in range(NT):
                last = nc.vector.tensor_tensor(pT[:, t, :], pT[:, t, :], rden[:], ALU.mult)
            last.then_inc(pTn_ready, 1)
            lo(0, 8)
            dve.wait_ge(hash_turned, 1)
            nc.vector.tensor_copy(hashT[:].rearrange("p c w -> p (c w)"), bank(7)[:, 0:C * PD])
            nc.vector.tensor_copy(keysT[:], bank(7)[0:PD, XP:2 * XP]).then_inc(hash_ready, 1)
            dve.wait_ge(zhi_ready, 1)
            nc.vector.tensor_tensor(zT_lo[:, :, 0:NH], high_cn[:, :, 0:NH], zT_hi[:, :, 0:NH].bitcast(F32),
                                    ALU.subtract)
            nc.vector.tensor_tensor(zT_lo[:, :, 2 * NH:PADZ], high_cn[:, :, NH:N],
                                    zT_hi[:, :, 2 * NH:PADZ].bitcast(F32), ALU.subtract).then_inc(zlo_ready, 1)
            lo(1, 8)
            lo(0, 9)
            lo(1, 9)
            lo(0, SLOT_W, down=True)
            dve.wait_ge(x_again, 16)
            for t in range(NT):
                if t == 0:
                    dve.wait_ge(nodes_done, 1)
                else:
                    dve.wait_ge(used[1], 2 * SLOT_W)
                nc.vector.scalar_tensor_tensor(out=xt[:, t, :], in0=bank(2 * t, 2), scalar=0.0,
                                               in1=xt[:, t, :], op0=ALU.max, op1=ALU.add).then_inc(x2_ready, 1)
                dve.wait_ge(x2_ready, t + 1)
                layer_norm(1, t)
            turn_lo(1)

            dve.wait_ge(hT_done, 1)
            nc.vector.tensor_copy(hT_sb[:], bank(1)[0:PD, 0:N]).then_inc(hT_copied, 1)
            dve.wait_ge(sim_done, 1)
            link(nc.vector.tensor_copy(sim[:], bank(2).rearrange("p (t n) -> p t n", t=NT)))
            for t in range(NT):
                last = nc.vector.max(top[:, t, :], sim[:, t, :])
            link(last)
            for t in range(NT):
                nc.vector.tensor_scalar(tope[:, t, TOPK:2 * TOPK], top[:, t, 0:TOPK], top[:, t, 0:1], None,
                                        ALU.subtract)
                last = nc.vector.max_index(topi[:, t, :], top[:, t, :], sim[:, t, :])
            last.then_inc(top_ready, 1)
            dve.wait_ge(top_ready, 1)
            link(nc.vector.tensor_copy(topf[:], topi[:]))
            dve.wait_ge(tope_ready, NT)
            link(nc.vector.reciprocal(tsum[:, :, 1], tsum[:, :, 0]))
            for t in range(NT):
                link(nc.vector.tensor_scalar(tope[:, t, 0:TOPK], tope[:, t, 0:TOPK], tsum[:, t, 1:2], None, ALU.mult))
                link(nc.vector.tensor_scalar(route[:, t, :], iota[:], topf[:, t, 0:1], tope[:, t, 0:1],
                                             ALU.is_equal, ALU.mult))
                for k in range(1, TOPK):
                    link(nc.vector.tensor_scalar(rtmp[:, t, :], iota[:], topf[:, t, k:k + 1], tope[:, t, k:k + 1],
                                                 ALU.is_equal, ALU.mult))
                    link(nc.vector.tensor_tensor(route[:, t, :], route[:, t, :], rtmp[:, t, :], ALU.add))

            def weigh(g):
                dve.wait_ge(silu_ready, g + 1)
                for t in range(NT):
                    w = route[:, t, bass.ds(g * GX, GX)].unsqueeze(2).to_broadcast([P, GX, PD])
                    last = nc.vector.tensor_tensor(gw[:, t, :].rearrange("p (n w) -> p n w", n=GX),
                                                   act_g[:, t, :].rearrange("p (n w) -> p n w", n=GX), w, ALU.mult)
                last.then_inc(gw_ready, 1)

            def gT_lo_part(g):
                dve.wait_ge(gThi_ready, g + 1)
                nc.vector.tensor_tensor(gT_lo[:].rearrange("p b n -> p (b n)"), bank(6, 2),
                                        gT_hi[:].rearrange("p b n -> p (b n)").bitcast(F32), ALU.subtract)\
                    .then_inc(gTlo_ready, 1)

            weigh(0)
            for t in range(NT):
                nc.vector.tensor_tensor(xt[:, t, :], xt[:, t, :], nf[:, t, :], ALU.add)
            lo(0, SLOT_W + 1, down=True)
            lo(1, SLOT_W)
            with dve.Fori(1, NG - 1) as g:
                gT_lo_part(g - 1)
                weigh(g)
                lo(0, g + (SLOT_W + 1), down=True)
                lo(1, g + SLOT_W)
            gT_lo_part(NG - 2)
            weigh(NG - 1)
            lo(0, LAST)
            gT_lo_part(NG - 1)
            for t in range(NT):
                dve.wait_ge(summed, t + 1)
                nc.vector.scalar_tensor_tensor(out=xt[:, t, :], in0=bank(2 * t, 2), scalar=scale_b[:, 0:1],
                                               in1=xt[:, t, :], op0=ALU.mult, op1=ALU.add).then_inc(out_ready, 1)

        @block.tensor
        def _(pe):
            def transpose(o, i):
                k = i.shape[0]
                return nc.tensor.transpose(o, i, ident[0:k, 0:k])

            def turn(k):
                for t in range(NT):
                    pe.wait_ge(norm_ready, k * NT + t + 1)
                    for c in range(C):
                        last = transpose(turned_cn[k][t][:, c, :],
                                         nf[:, t, :].rearrange("p (q c) -> p c q", c=C)[:, c, :])
                    last.then_inc(turned, 1)

            pe.wait_ge(consts, 14)
            pe.wait_ge(norm_ready, NT)
            pe.wait_ge(picker_ready, 1)
            for h in range(2):
                for c in range(C):
                    for t in range(NT):
                        last = nc.tensor.matmul(bank(4 + 2 * h, 2)[:, c * P:(c + 1) * P],
                                                nf[:, t, :].rearrange("p (q c) -> p c q", c=C)[:, c, :],
                                                onehot[:, 1, 2 * h + t, 0:P].bitcast(F32),
                                                start=t == 0, stop=t == NT - 1)
                last.then_inc(feat_done, 1)
            turn(0)
            pe.wait_ge(idx_float, 1)
            pe.wait_ge(featlo_ready, 1)
            for a in range(2):
                transpose(bank(4)[:, a * ET:(a + 1) * ET], idx_rowf[:, a, :])
            transpose(bank(5)[0:1, 0:EG], group_ends[:, 4:5]).then_inc(smallT, 1)

            def three(o, a_hi, a_lo, b_hi, b_lo, start, stop):
                nc.tensor.matmul(o, a_hi, b_hi, start=start, stop=False)
                nc.tensor.matmul(o, a_lo, b_hi, start=False, stop=False)
                return nc.tensor.matmul(o, a_hi, b_lo, start=False, stop=stop)

            def add_bias(o, rows, g, start=True, stop=False):
                cols = slice(g * HALF, (g + 1) * HALF)
                nc.tensor.matmul(o, rows, bias_hi[:, cols], start=start, stop=False)
                return nc.tensor.matmul(o, rows, bias_lo[:, cols], start=False, stop=stop)

            w_hi = [whi[:, s, :].rearrange("p (c n) -> p c n", c=4) for s in range(2)]
            w_lo = [wlo[:, s, :].rearrange("p (c n) -> p c n", c=4) for s in range(2)]

            def gather(q, s, odd, quarters=(0, 1, 2, 3), first=None):
                for c in quarters:
                    if first is not None:
                        pe.wait_ge(tablo_ready, 4 * (first - 1) + c + 1)
                    for h in range(2):
                        for part, tab in enumerate((tab_hi, tab_lo)):
                            last = nc.tensor.matmul(bank(2 * q + h), onehot[:, s, c, odd * P:(odd + 1) * P],
                                                    tab[:, c, h * HALF:(h + 1) * HALF],
                                                    start=c == 0 and part == 0,
                                                    stop=c == quarters[-1] and part == 1)
                last.then_inc(gathered, 1)

            def project(k, h):
                if h == 1:
                    for t in range(NT):
                        for g in range(2):
                            add_bias(bank(4 + 2 * t + g), sel[:, k, :], g)
                for s in range(2):
                    for cc in range(4):
                        if cc % 2 == 0:
                            pe.wait_ge(lo_ready[s], 2 * (2 * k + h) + cc // 2 + 1)
                        c = 4 * s + cc
                        for t in range(NT):
                            for g in range(2):
                                last = three(bank(4 * h + 2 * t + g), tokens(nT_hi, c, t), tokens(nT_lo, c, t),
                                             w_hi[s][:, cc, g * HALF:(g + 1) * HALF],
                                             w_lo[s][:, cc, g * HALF:(g + 1) * HALF],
                                             start=h == 0 and c == 0, stop=c == C - 1)
                            if c == C - 1 and t == 0:
                                last.then_inc(table_done, 1)
                        if cc % 2 == 1:
                            last.then_inc(used[s], 1)

            pe.wait_ge(bias_ready, 2)
            pe.wait_ge(featlo_ready, 2)
            for h in range(2):
                for s in range(2):
                    for cc in range(4):
                        if cc % 2 == 0:
                            pe.wait_ge(lo_ready[s], 2 * h + cc // 2 + 1)
                        c = 4 * s + cc
                        for g in range(2):
                            last = three(bank(6 + g), feat_hi[:, C * h + c, :], feat_lo[:, C * h + c, :],
                                         w_hi[s][:, cc, g * HALF:(g + 1) * HALF],
                                         w_lo[s][:, cc, g * HALF:(g + 1) * HALF],
                                         start=h == 0 and c == 0, stop=False)
                        if cc % 2 == 1:
                            last.then_inc(used[s], 1)
            for g in range(2):
                last = add_bias(bank(6 + g), sel[:, 0, :], g, start=False, stop=True)
            last.then_inc(gathered, 1)

            pe.wait_ge(turned_lo, NT)
            pe.wait_ge(small_ready, 1)
            for k in (1, 2):
                if k == 2:
                    pe.wait_ge(dot_done, FIRST_TILE[2])
                project(k, 0)
                if k == 1:
                    pe.wait_ge(dot_done, 1)
                project(k, 1)
                for i in range(FIRST_TILE[k], min(FIRST_TILE[k + 1], 2 * GROUP)):
                    pe.wait_ge(onehot_ready, i // 2 + 1)
                    if i >= 4:
                        pe.wait_ge(dot_done, i - 3)
                    gather(pair_of(i), (i // 2) % 2, i % 2, first=k if i == FIRST_TILE[k] else None)

            def gather_group(it, quarters):
                for j in range(GROUP):
                    pe.wait_ge(onehot_ready, 2 * it + 5 + j // 2)
                    pe.wait_ge(dot_done, 4 * it + 5 + j)
                    gather(pair_of(2 * GROUP + j), j // 2, j % 2, quarters)

            with pe.Fori(0, EG - 2) as it:
                which = pe.value_load(halves[0:1, bass.ds(it + 2, 1)], min_val=1, max_val=3)
                with pe.If(which == 1):
                    gather_group(it, (0, 1, 2))
                with pe.If(which == 2):
                    gather_group(it, (0, 1, 3))
                with pe.If(which == 3):
                    gather_group(it, (0, 1, 2, 3))

            pe.wait_ge(dot_done, ET)
            sel_cols = sel[:].rearrange("q b n -> q (b n)")
            for t, first in enumerate((3 * P + NH, 4 * P)):
                for g in range(2):
                    add_bias(bank(2 * t + g), sel_cols[:, first:first + P], g)

            def new_nodes(aT_hi, aT_lo, columns, u, first_kind, stop=False, parts=(0, 1)):
                s = u % 2
                for j in parts:
                    pe.wait_ge(lo_ready[s], 2 * (u // 2) + j + 1)
                    for t, at in enumerate(columns[:1] if first_kind else columns[1:]):
                        for cc in (2 * j, 2 * j + 1):
                            c = 4 * s + cc
                            for g in range(2):
                                last = three(bank(2 * t + g), aT_hi[:, c, at:at + P], aT_lo[:, c, at:at + P],
                                             w_hi[s][:, cc, g * HALF:(g + 1) * HALF],
                                             w_lo[s][:, cc, g * HALF:(g + 1) * HALF],
                                             start=False, stop=stop and c == C - 1)
                        if stop and j == 1 and t == 0:
                            last.then_inc(nodes_done, 1)
                    last.then_inc(used[s], 1)

            own = (2 * NH, 0, 4 * NH)
            messages = (0, NH, 3 * NH)
            new_nodes(nT_hi, nT_lo, own, 12, True)
            new_nodes(nT_hi, nT_lo, own, 13, True)
            new_nodes(nT_hi, nT_lo, own, 14, False)

            def pair(i, s, start=False, stop=False):
                pe.wait_ge(oh_ready, i + 1)
                rows = oh_src[:, bass.ds(i, 1), :].rearrange("p a n -> p (a n)")
                for t in range(NT):
                    for part in range(2):
                        last = nc.tensor.matmul(bank(4 + t)[:, 0:N], rows[:, t * P:(t + 1) * P],
                                                oh_dst[:, s, part, :], start=start and part == 0,
                                                stop=stop and part == 1)
                last.then_inc(paired, 1)

            pe.wait_ge(src_act, ACT_TILES)
            for s in range(OB):
                pair(s, s, start=s == 0)
            with pe.Fori(1, ACT_TILES // OB) as m:
                for s in range(OB):
                    pair(OB * m + s, s)
            with pe.Fori(ACT_TILES // OB, ET // OB - 1) as m:
                pe.wait_ge(src_pool, OB * m + (OB - ACT_TILES))
                for s in range(OB):
                    pair(OB * m + s, s)
            pe.wait_ge(src_pool, POOL_TILES)
            for s in range(OB):
                pair(ET - OB + s, s, stop=s == OB - 1)
            pe.wait_ge(pT_ready, 1)
            pe.wait_ge(pool_chain, 3)
            for t in range(NT):
                last = nc.tensor.matmul(bank(6)[:, 0:N], ones[:], pT[:, t, :], start=t == 0, stop=t == NT - 1)
            last.then_inc(den_ready, 1)
            pe.wait_ge(hash_loaded, 32)
            for c in range(C):
                transpose(bank(7)[:, c * PD:(c + 1) * PD], hash_w[:].rearrange("w (q c) -> w c q", c=C)[:, c, :])
            for t in range(NT):
                last = transpose(bank(7)[0:PD, XP + t * P:XP + (t + 1) * P], keys_n[:, t, :])
            last.then_inc(hash_turned, 1)
            new_nodes(nT_hi, nT_lo, own, 15, False, parts=(0,))
            pe.wait_ge(hash_ready, 1)
            pe.wait_ge(pTn_ready, 1)
            for c in range(C):
                for t in range(NT):
                    last = nc.tensor.matmul(high_cn[:, c, :], nf[:, t, :].rearrange("p (q c) -> p c q", c=C)[:, c, :],
                                            pT[:, t, :], start=t == 0, stop=t == NT - 1)
            last.then_inc(z_ready, 1)
            new_nodes(nT_hi, nT_lo, own, 15, False, parts=(1,))
            pe.wait_ge(zlo_ready, 1)
            pe.wait_ge(z_zeroed, 2)
            new_nodes(zT_hi, zT_lo, messages, 16, True)
            new_nodes(zT_hi, zT_lo, messages, 17, True)
            new_nodes(zT_hi, zT_lo, messages, 18, False)
            new_nodes(zT_hi, zT_lo, messages, 19, False, stop=True)

            turn(1)
            pe.wait_ge(turned_lo, 2 * NT)
            for c in range(C):
                for part, aT in enumerate((nT_hi, nT_lo)):
                    last = nc.tensor.matmul(bank(1)[0:PD, 0:N], hashT[:, c, :], aT[:, c, 2 * NH:PADN].bitcast(F32),
                                            start=c == 0 and part == 0, stop=c == C - 1 and part == 1)
            last.then_inc(hT_done, 1)
            pe.wait_ge(hT_copied, 1)
            for t in range(NT):
                last = nc.tensor.matmul(bank(2)[:, t * N:(t + 1) * N], hT_sb[:, t * P:(t + 1) * P], keysT[:],
                                        start=True, stop=True)
            last.then_inc(sim_done, 1)

            down_hi = whi[:, 0, :].rearrange("p (n c w) -> p c n w", n=GX, c=C)
            down_lo = wlo[:, 0, :].rearrange("p (n c w) -> p c n w", n=GX, c=C)

            def down(g):
                for c in range(C):
                    if c % 4 == 0:
                        pe.wait_ge(lo_ready[0], 2 * g + (2 * SLOT_W + c // 4 + 1))
                    for t in range(NT):
                        cols = slice((2 + 2 * t) * NH, (4 + 2 * t) * NH)
                        last = three(bank(4 + t), nT_hi[:, c, cols], nT_lo[:, c, cols],
                                     down_hi[:, c, :, :], down_lo[:, c, :, :], start=c == 0, stop=c == C - 1)
                    if c % 4 == 3:
                        last.then_inc(used[0], 1)

            def turn_group(g):
                pe.wait_ge(gw_ready, g + 1)
                for b in range(BLOCKS):
                    for t in range(NT):
                        last = transpose(ps[:, 6 * HALF + b * N + t * P:6 * HALF + b * N + (t + 1) * P],
                                         gw[:, t, b * P:(b + 1) * P])
                last.then_inc(gT_done, 1)

            def up_block(s, b, t, stop=False):
                for h in range(2):
                    last = three(bank(2 * t + h), gT_hi[:, b, t * P:(t + 1) * P], gT_lo[:, b, t * P:(t + 1) * P],
                                 w_hi[s][:, b, h * HALF:(h + 1) * HALF], w_lo[s][:, b, h * HALF:(h + 1) * HALF],
                                 start=False, stop=stop)
                return last

            def up(g):
                pe.wait_ge(gTlo_ready, g + 1)
                for b in range(BLOCKS):
                    if b % 2 == 0:
                        pe.wait_ge(lo_ready[1], 2 * g + (2 * SLOT_W + b // 2 + 1))
                    for t in range(NT):
                        last = up_block(1, b, t)
                    if b % 2 == 1:
                        last.then_inc(used[1], 1)

            down(0)
            turn_group(0)
            for b in range(4):
                nc.tensor.matmul(bank(b), sel[0:1, 1, :], sel_cols[0:1, P:P + HALF], start=True, stop=False)
            with pe.Fori(1, NG) as g:
                pe.wait_ge(silu_ready, g)
                down(g)
                up(g - 1)
                turn_group(g)
            pe.wait_ge(gTlo_ready, NG)
            pe.wait_ge(lo_ready[0], 2 * LAST + 2)
            for t in range(NT):
                for b in range(BLOCKS):
                    last = up_block(0, b, t, stop=b == BLOCKS - 1)
                last.then_inc(summed, 1)



_INS = ['x', 'src', 'dst', 'L0_gnn_W_hh', 'L0_gnn_b_hh', 'L0_gnn_W_oo', 'L0_gnn_b_oo', 'L0_gnn_W_ho', 'L0_gnn_b_ho',
        'L0_gnn_W_a', 'L0_gnn_b_a', 'L0_gnn_W_hn', 'L0_gnn_b_hn', 'L0_gnn_W_on', 'L0_gnn_b_on', 'L0_ffn_hasher_w',
        'L0_ffn_keys', 'L0_ffn_values_down', 'L0_ffn_values_up', 'L0_ffn_scale']


def kernel(**inputs):
    import numpy as _np
    import concourse.bacc as _bacc
    from concourse import mybir as _mybir
    from concourse.bass_utils import run_bass_kernel_spmd as _run

    nc = _bacc.Bacc("TRN2", target_bir_lowering=False, num_devices=1)
    arrays, args = {}, []
    for name in _INS:
        a = _np.ascontiguousarray(inputs[name])
        arrays[f"in_{name}_dram"] = a
        args.append(nc.dram_tensor(f"in_{name}_dram", a.shape, _mybir.dt.from_np(a.dtype), kind="ExternalInput").ap())
    out = nc.dram_tensor("out_0_dram", (N, D), _mybir.dt.float32, kind="ExternalOutput").ap()
    gnn_ffn(nc, *args, out)
    r = _run(nc, [arrays], core_ids=[0])
    return r.results[0]["out_0_dram"]
```

```python
from contextlib import ExitStack

import concourse.bass as bass
from concourse import mybir
from concourse.alu_op_type import AluOpType as ALU

F32 = mybir.dt.float32
F32R = mybir.dt.float32r
BF16 = mybir.dt.bfloat16
F16 = mybir.dt.float16
I32 = mybir.dt.int32
U32 = mybir.dt.uint32
ACT = mybir.ActivationFunctionType
RMAX = bass.bass_isa.ReduceOp.max

P = 128
N = 256
NT = N // P
D = 1024
C = D // P
HALF = 512
NH = 64
PADN = N + 2 * NH
PADZ = N + NH
E = 8192
ET = E // P
FIRST_TILE = [0, 1, 6, ET]
BATCH = 2 * P
NB = E // BATCH
STACK_BASE = (64, 0, 128, 192)
STACK_HI = (0, 64, 0, 64)
SPANS = ((1,), (0,), (2,), (3,), (1, 0), (0, 2), (2, 3))
GROUP = 4
EG = ET // GROUP
OB = 8
HEAD_START = 4
POOL_TILES = 40
ACT_TILES = ET - POOL_TILES
ACT_HEAD = 8
XP = 256
PD = 32
TOPK = 4
GX = 16
NG = XP // GX
UNIT = 4096
WUNITS = 20
SLOT_W = WUNITS // 2
LAST = SLOT_W + NG
EPS = 1e-5
NEVER = -3.0e38
BLOCKS = GX * PD // P


def gnn_ffn(nc, x, src, dst, W_hh, b_hh, W_oo, b_oo, W_ho, b_ho, W_a, b_a, W_hn, b_hn, W_on, b_on,
            hasher_w, keys, values_down, values_up, scale, out):
    ctx = ExitStack()
    with ctx:
        def sb(name, shape, dt=F32, where=ctx):
            return where.enter_context(nc.sbuf_tensor(name, shape, dt))

        def sem(name):
            return ctx.enter_context(nc.semaphore(name))

        raw = sb("raw", [P, 2, UNIT])
        whi = sb("whi", [P, 2, UNIT], F32R)
        wlo = sb("wlo", [P, 2, UNIT], F32R)
        xt = sb("xt", [P, NT, D])
        wa_b = xt[:, 1, :]
        nf = sb("nf", [P, NT, D])
        nT_hi = sb("nT_hi", [P, C, PADN], F32R)
        nT_lo = sb("nT_lo", [P, C, PADN], F32R)
        iota = sb("iota", [P, N])
        iota16 = sb("iota16", [P, N], F16)
        node = sb("node", [P, 2])
        stack_neg = sb("stack_neg", [P, 4])
        spare = sb("spare", [P, 1])
        row_no = sb("row_no", [P, 1])
        ident = sb("ident", [P, P])
        sel = sb("sel", [5, 5, P], F32R)
        sel_ones = sb("sel_ones", [5, 1])
        bias_hi = sb("bias_hi", [5, D], F32R)
        bias_lo = sb("bias_lo", [5, D], F32R)
        segmax = sb("segmax", [P, N])
        segall = sb("segall", [P, N])
        logit = sb("logit", [P, ET])
        peak = sb("peak", [P, ET])
        ex = sb("ex", [P, ET])
        ex_16 = sb("ex_16", [P, ET], F16)
        ex_hi = sb("ex_hi", [P, ET])
        ex_lo = sb("ex_lo", [P, ET])
        idx_neg = sb("idx_neg", [P, 2, ET])
        idx_col = sb("idx_col", [P, 2, ET])
        scale_b = sb("scale_b", [P, 1])
        ba_b = sb("ba_b", [P, 1])
        stats = sb("stats", [P, NT, 2, 6])
        mv = sb("mv", [P, NT, 2])
        ln = sb("ln", [P, 5, NT])
        with ExitStack() as early:
            idx_rows = sb("idx_rows", [ET, 2, P], I32, early)
            idx_rowf = sb("idx_rowf", [ET, 2, P], F32, early)
            group_ends = sb("group_ends", [EG, 11], F32, early)
            bias = sb("bias", [5, D], F32, early)
        spans = sb("spans", [1, EG], I32)
        with ExitStack() as edge:
            tab_hi = sb("tab_hi", [P, NT, D], F32R, edge)
            tab_lo = sb("tab_lo", [P, NT, D], F32R, edge)
            tab_dst = sb("tab_dst", [P, 4, D], F32R, edge)
            onehot = sb("onehot", [P, 2, 6, BATCH], F32R, edge)
            node_gap = sb("node_gap", [P, 4, BATCH], F16, edge)
            idx_b = sb("idx_b", [P, 2, 2, BATCH], I32, edge)
            junk = sb("junk", [P, D], BF16, edge)
            pen = sb("pen", [P, N], F32, edge)
        group_rows = junk[0:EG, :].bitcast(I32)
        feat_hi = tab_dst[:, 0:2, :].rearrange("p a (c e) -> p (a c) e", e=P)
        feat_lo = tab_dst[:, 2:4, :].rearrange("p a (c e) -> p (a c) e", e=P)
        ones = sb("ones", [P, P])
        hash_w = sb("hash_w", [PD, D])
        hashT = sb("hashT", [P, C, PD])
        keys_n = sb("keys_n", [P, NT, PD])
        keysT = sb("keysT", [PD, XP])
        with ExitStack() as late:
            pT = sb("pT", [P, NT, N], F32, late)
            rden = sb("rden", [P, N], F32, late)
            with ExitStack() as pairs:
                junk2 = sb("junk2", [P, 4, N], BF16, pairs)
                distance = sb("distance", [P, 4, N], F16, pairs)
                oh_src = sb("oh_src", [P, ET, N], F16, pairs)
                oh_dst = sb("oh_dst", [P, OB, 2, N], F16, pairs)
            zT_hi = sb("zT_hi", [P, C, PADZ], F32R, late)
            zT_lo = sb("zT_lo", [P, C, PADZ], F32R, late)
        hT_sb = sb("hT_sb", [PD, N])
        sim = sb("sim", [P, NT, XP])
        top = sb("top", [P, NT, 8])
        topi = sb("topi", [P, NT, 8], U32)
        topf = sb("topf", [P, NT, 8])
        tope = sb("tope", [P, NT, 8])
        tsum = sb("tsum", [P, NT, 2])
        route = sb("route", [P, NT, XP])
        rtmp = sb("rtmp", [P, 2, XP])
        act_g = sb("act_g", [P, NT, GX * PD])
        gw = sb("gw", [P, NT, GX * PD])
        gT_hi = sb("gT_hi", [P, BLOCKS, N], F32R)
        gT_lo = sb("gT_lo", [P, BLOCKS, N], F32R)
        gT_last_hi = sb("gT_last_hi", [P, BLOCKS, N], F32R)
        gT_last_lo = sb("gT_last_lo", [P, BLOCKS, N], F32R)

        ps = ctx.enter_context(nc.psum_tensor("ps", [P, 8 * HALF], F32))

        def bank(b, n=1):
            return ps[:, b * HALF:(b + n) * HALF]

        turned_cn = [[bank(4 * k + 2 * t, 2).rearrange("p (c n) -> p c n", c=C) for t in range(NT)]
                     for k in range(2)]
        high_cn = bank(4, 4).rearrange("p (c n) -> p c n", c=C)

        x_loaded = [sem(f"x_loaded{t}") for t in range(NT)]
        idx_loaded = sem("idx_loaded")
        small_loaded = sem("small_loaded")
        edge_loaded = sem("edge_loaded")
        batch_loaded = [sem(f"batch_loaded{s}") for s in range(2)]
        loaded = [sem(f"loaded{s}") for s in range(2)]
        hi_ready = [sem(f"hi_ready{s}") for s in range(2)]
        lo_ready = [sem(f"lo_ready{s}") for s in range(2)]
        used = [sem(f"used{s}") for s in range(2)]
        consts = sem("consts")
        pool_chain = sem("pool_chain")
        chain = sem("chain")
        var_ready = sem("var_ready")
        root_ready = sem("root_ready")
        norm_ready = sem("norm_ready")
        turned = sem("turned")
        turned_hi = sem("turned_hi")
        turned_lo = sem("turned_lo")
        picker_ready = sem("picker_ready")
        feat_done = sem("feat_done")
        feathi_ready = sem("feathi_ready")
        featlo_ready = sem("featlo_ready")
        idx_float = sem("idx_float")
        group_loaded = sem("group_loaded")
        smallT = sem("smallT")
        small_ready = sem("small_ready")
        table_done = sem("table_done")
        tabhi_ready = sem("tabhi_ready")
        tablo_ready = sem("tablo_ready")
        onehot_ready = sem("onehot_ready")
        gap_ready = sem("gap_ready")
        onehot_dst = sem("onehot_dst")
        gathered = sem("gathered")
        pen_ready = sem("pen_ready")
        dot_done = sem("dot_done")
        seg_done = sem("seg_done")
        segall_ready = sem("segall_ready")
        peak_done = sem("peak_done")
        diff_ready = sem("diff_ready")
        ex_ready = sem("ex_ready")
        src_pool = sem("src_pool")
        distance_ready = sem("distance_ready")
        src_act = sem("src_act")
        ex_split = sem("ex_split")
        oh_ready = sem("oh_ready")
        oh_act = sem("oh_act")
        z_zeroed = sem("z_zeroed")
        bias_ready = sem("bias_ready")
        x_again = sem("x_again")
        hash_loaded = sem("hash_loaded")
        hash_turned = sem("hash_turned")
        hash_ready = sem("hash_ready")
        paired = sem("paired")
        pT_ready = sem("pT_ready")
        den_ready = sem("den_ready")
        pTn_ready = sem("pTn_ready")
        z_ready = sem("z_ready")
        zhi_ready = sem("zhi_ready")
        zlo_ready = sem("zlo_ready")
        nodes_done = sem("nodes_done")
        x2_ready = sem("x2_ready")
        hT_done = sem("hT_done")
        hT_copied = sem("hT_copied")
        sim_done = sem("sim_done")
        top_ready = sem("top_ready")
        tope_ready = sem("tope_ready")
        silu_ready = sem("silu_ready")
        gw_ready = sem("gw_ready")
        gT_done = sem("gT_done")
        gThi_ready = sem("gThi_ready")
        gTlo_ready = sem("gTlo_ready")
        summed = sem("summed")
        out_ready = sem("out_ready")
        stored = sem("stored")

        def pair_of(i):
            return (3, 0, 1, 2, 3, 2)[i] if i < FIRST_TILE[2] else (i - FIRST_TILE[2]) % 4

        def rows(w, half, quarter):
            v = w[half * D:(half + 1) * D, :].rearrange("(p c) n -> p c n", c=C)
            return v[:, 4 * quarter:4 * quarter + 4, :]

        unit_source = [rows(w, h, q) for w in (W_hh, W_oo, W_ho) for h in range(2) for q in range(2)]
        unit_source += [rows(w, h, q) for h in range(2) for w in (W_hn, W_on) for q in range(2)]
        down_v = values_down.rearrange("n (p c) w -> p n (c w)", c=C)
        up_v = values_up.rearrange("n w d -> (n w) d").rearrange("(b q) d -> q b d", q=P)
        raw_down = raw[:, 0, :].rearrange("p (n k) -> p n k", n=GX)
        raw_up = [raw[:, s, :].rearrange("p (b d) -> p b d", b=BLOCKS) for s in range(2)]

        def half(t, s, j, down=False):
            if down:
                return t[:, s, :].rearrange("p (n k) -> p n k", n=GX)[:, :, j * 4 * PD:(j + 1) * 4 * PD]
            return t[:, s, j * UNIT // 2:(j + 1) * UNIT // 2]

        def tokens(t3, c, t):
            return t3[:, c, NH:NH + P] if t == 0 else t3[:, c, 4 * NH:PADN]

        def token_columns(k, t):
            if t == 1:
                return ((4 * NH, 0, P),)
            return ((NH, NH, NH), (2 * NH, 0, NH)) if k == 0 else ((2 * NH, 0, P),)

        block = ctx.enter_context(nc.Block())

        @block.sync
        def _(sp):
            x_v = x.rearrange("(t p) n -> p t n", p=P)
            for t in range(NT):
                sp.dma_start(xt[:, t, :], x_v[:, t, :]).then_inc(x_loaded[t], 16)
            for u in range(WUNITS):
                s, n = u % 2, u // 2
                if n:
                    sp.wait_ge(lo_ready[s], 2 * n)
                if u == 16:
                    sp.wait_ge(seg_done, ET)
                    sp.dma_start(xt[:, 1, :], x_v[:, 1, :]).then_inc(x_again, 16)
                    sp.dma_start(hash_w[:], hasher_w).then_inc(hash_loaded, 16)
                    sp.dma_start(keys_n[:], keys.rearrange("(t p) w -> p t w", p=P)).then_inc(hash_loaded, 16)
                dst_ap = raw[:, s, :].rearrange("p (c n) -> p c n", c=4)
                sp.dma_start(dst_ap, unit_source[u]).then_inc(loaded[s], 16)
            sp.wait_ge(lo_ready[0], 2 * SLOT_W)
            sp.dma_start(raw_down, down_v[:, 0:GX, :]).then_inc(loaded[0], 16)
            with sp.Fori(0, NG - 1) as g:
                sp.wait_ge(lo_ready[0], 2 * g + 2 * (SLOT_W + 1))
                sp.dma_start(raw_down, down_v[:, bass.ds((g + 1) * GX, GX), :]).then_inc(loaded[0], 16)
                sp.wait_ge(lo_ready[1], 2 * g + 2 * SLOT_W)
                sp.dma_start(raw_up[1], up_v[:, bass.ds(g * BLOCKS, BLOCKS), :]).then_inc(loaded[1], 16)
            sp.wait_ge(lo_ready[0], 2 * LAST)
            sp.dma_start(raw_up[0], up_v[:, (NG - 1) * BLOCKS:NG * BLOCKS, :]).then_inc(loaded[0], 16)
            out_v = out.rearrange("(t p) n -> p t n", p=P)
            for n in range(2 * NT):
                t, cols = n // 2, slice((n % 2) * HALF, (n % 2 + 1) * HALF)
                sp.wait_ge(out_ready, n + 1)
                sp.dma_start(out_v[:, t, cols], xt[:, t, cols]).then_inc(stored, 16)
            sp.wait_ge(stored, 16 * 2 * NT)

        @block.gpsimd
        def _(pool):
            def load_batch(b, s):
                pool.dma_start(idx_b[:, s, 0, :], src[bass.ds(b * BATCH, BATCH)].partition_broadcast(P))\
                    .then_inc(batch_loaded[s], 16)
                pool.dma_start(idx_b[:, s, 1, :], dst[bass.ds(b * BATCH, BATCH)].partition_broadcast(P))\
                    .then_inc(batch_loaded[s], 16)

            load_batch(0, 0)
            load_batch(1, 1)
            made = [0]

            def constant(ins):
                made[0] += 1
                ins.then_inc(consts, 1)
                pool.wait_ge(consts, made[0])

            nc.gpsimd.memset(ident[:], 0.0).then_inc(pool_chain, 1)
            nc.gpsimd.memset(sel_ones[:], 1.0).then_inc(pool_chain, 1)
            pool.wait_ge(pool_chain, 2)
            constant(nc.gpsimd.affine_select(out=ident[:], in_=ident[:], compare_op=ALU.not_equal, fill=1.0,
                                             base=0, pattern=[[-1, P]], channel_multiplier=1))
            for col, part, base in ((0, 0, NH), (0, NH, 0), (1, 0, P), (1, NH, P + NH)):
                constant(nc.gpsimd.iota(node[part:part + NH, col:col + 1], pattern=[[0, 1]], base=base,
                                        channel_multiplier=1, allow_small_or_imprecise_dtypes=True))
            constant(nc.gpsimd.iota(row_no[:], pattern=[[0, 1]], base=0, channel_multiplier=1,
                                    allow_small_or_imprecise_dtypes=True))
            constant(nc.gpsimd.affine_select(out=sel[:], in_=sel_ones[:].unsqueeze(2).to_broadcast([5, 5, P]),
                                             compare_op=ALU.is_equal, fill=0.0, base=0, pattern=[[-1, 5], [0, P]],
                                             channel_multiplier=1))
            for T in (nT_hi, nT_lo):
                for at in (0, 3 * NH):
                    constant(nc.gpsimd.memset(T[:, :, at:at + NH].bitcast(F32), 0.0))
            constant(nc.gpsimd.iota(iota[:], pattern=[[1, N]], base=0, channel_multiplier=0,
                                    allow_small_or_imprecise_dtypes=True))
            constant(nc.gpsimd.tensor_copy(iota16[:], iota[:]))
            constant(nc.gpsimd.memset(segmax[:], NEVER))
            for q, base in enumerate(STACK_BASE):
                for part in (0, NH):
                    constant(nc.gpsimd.iota(stack_neg[part:part + NH, q:q + 1], pattern=[[0, 1]], base=-base,
                                            channel_multiplier=-1, allow_small_or_imprecise_dtypes=True))

            with pool.Fori(1, NB // 2) as i:
                for s in range(2):
                    pool.wait_ge(onehot_ready, 2 * i - 1 + s)
                    pool.wait_ge(onehot_dst, 2 * i - 1 + s)
                    load_batch(2 * i + s, s)

            def pool_lo(s, n, parts=(0, 1), down=False):
                for j in parts:
                    pool.wait_ge(hi_ready[s], 2 * n + j + 1)
                    nc.gpsimd.tensor_tensor(half(wlo, s, j, down), half(raw, s, j, down),
                                            half(whi, s, j, down).bitcast(F32), ALU.subtract)\
                        .then_inc(lo_ready[s], 1)

            pool_lo(1, 6)
            pool.wait_ge(seg_done, ET)
            nc.gpsimd.partition_all_reduce(segall[:], segmax[:], P, RMAX).then_inc(segall_ready, 1)
            for i in range(POOL_TILES):
                if i == HEAD_START:
                    pool_lo(0, 7)
                    pool_lo(1, 7, parts=(0,))
                nc.gpsimd.tensor_scalar(oh_src[:, ACT_TILES + i, :], iota16[:],
                                        idx_col[:, 0, ACT_TILES + i:ACT_TILES + i + 1], None,
                                        ALU.is_equal).then_inc(src_pool, 1)
            pool_lo(1, 7, parts=(1,))
            nc.gpsimd.memset(ones[:], 1.0).then_inc(pool_chain, 1)
            pool.wait_ge(paired, ET)
            nc.gpsimd.memset(zT_hi[:, :, NH:2 * NH].bitcast(F32), 0.0).then_inc(z_zeroed, 1)
            nc.gpsimd.memset(zT_lo[:, :, NH:2 * NH].bitcast(F32), 0.0).then_inc(z_zeroed, 1)
            pool_lo(0, SLOT_W, down=True)
            pool_lo(0, SLOT_W + 1, parts=(0,), down=True)

        @block.scalar
        def _(act):
            act.dma_start(group_rows, dst.rearrange("(g n) -> g n", g=EG)).then_inc(group_loaded, 16)
            act.dma_start(idx_rows[:, 0, :], src.rearrange("(t p) -> t p", p=P)).then_inc(idx_loaded, 16)
            act.dma_start(idx_rows[:, 1, :], dst.rearrange("(t p) -> t p", p=P)).then_inc(idx_loaded, 16)
            def root(k, first, last):
                act.wait_ge(var_ready, k)
                nc.scalar.activation(ln[:, 1, first:last], ln[:, 0, first:last], ACT.Sqrt).then_inc(root_ready, 1)

            def turn_hi(k):
                for t in range(NT):
                    act.wait_ge(turned, NT * k + t + 1)
                    for to, at, w in token_columns(k, t):
                        last = nc.scalar.activation(nT_hi[:, :, to:to + w], turned_cn[k][t][:, :, at:at + w], ACT.Copy)
                    last.then_inc(turned_hi, 1)

            def hi(s, n, first=False, down=False, other=False, parts=(0, 1)):
                act.wait_ge(loaded[s], 16 * n + 16)
                for j in parts:
                    if not first:
                        act.wait_ge(used[s], 2 * n + (0 if other else j - 1))
                    nc.scalar.activation(half(whi, s, j, down), half(raw, s, j, down), ACT.Copy)\
                        .then_inc(hi_ready[s], 1)

            root(1, 0, NT)
            for q, b in enumerate((b_hh, b_oo, b_ho, b_hn, b_on)):
                act.dma_start(bias[q:q + 1, :], b.rearrange("(a n) -> a n", a=1)).then_inc(small_loaded, 16)
            act.dma_start(scale_b[:], scale.partition_broadcast(P)).then_inc(small_loaded, 16)
            act.dma_start(ba_b[:], b_a.partition_broadcast(P)).then_inc(edge_loaded, 16)
            act.wait_ge(norm_ready, NT)
            act.dma_start(wa_b, W_a.rearrange("n a -> (n a)").partition_broadcast(P)).then_inc(edge_loaded, 16)
            hi(0, 0, first=True)
            act.wait_ge(small_loaded, 16 * 6)
            nc.scalar.activation(bias_hi[:], bias[:], ACT.Copy).then_inc(bias_ready, 1)
            for h in range(2):
                act.wait_ge(feat_done, h + 1)
                nc.scalar.activation(feat_hi[:, C * h:C * h + C, :].rearrange("p c e -> p (c e)"),
                                     bank(4 + 2 * h, 2), ACT.Copy).then_inc(feathi_ready, 1)
            hi(1, 0, first=True)
            turn_hi(0)
            hi(0, 1)
            hi(1, 1)
            hi(0, 2)

            def stack_onehot(b, s):
                for q in range(4):
                    nc.scalar.activation(node_gap[:, q, :], idx_b[:, s, 1, :], ACT.Abs,
                                         bias=stack_neg[:, q:q + 1]).then_inc(gap_ready, 1)
                for q in range(4):
                    act.wait_ge(gap_ready, 4 * b + (q + 1))
                    last = nc.scalar.activation(onehot[:, s, 2 + q, :], node_gap[:, q, :], ACT.Relu,
                                                bias=1.0, scale=-1.0)
                last.then_inc(onehot_dst, 1)

            act.wait_ge(consts, 22)
            for b in range(2):
                act.wait_ge(batch_loaded[b], 32)
                if b:
                    act.wait_ge(onehot_dst, b)
                stack_onehot(b, b)

            def table_hi(k, h):
                for t in range(NT):
                    if t == 0:
                        act.wait_ge(table_done, 2 * (k - 1) + h + 1)
                    else:
                        act.wait_ge(used[1], 4 * k + 2 * h + 2)
                    act.wait_ge(gathered, FIRST_TILE[k])
                    if h == 0:
                        nc.scalar.activation(tab_hi[:, t, :], bank(2 * t, 2), ACT.Copy).then_inc(tabhi_ready, 1)
                    else:
                        for q in (2 * t, 2 * t + 1):
                            at = STACK_HI[q]
                            nc.scalar.activation(tab_dst[at:at + NH, q, :], bank(4 + 2 * t, 2)[at:at + NH, :],
                                                 ACT.Copy).then_inc(tabhi_ready, 1)

            for k in (1, 2):
                hi(1, 2 * k)
                hi(0, 2 * k + 1)
                table_hi(k, 0)
                hi(1, 2 * k + 1)
                hi(0, 2 * k + 2)
                table_hi(k, 1)
                for b in range((FIRST_TILE[k] + 4) // 2, (min(FIRST_TILE[k + 1], 8) + 4) // 2):
                    act.wait_ge(batch_loaded[b % 2], 32 * (b // 2 + 1))
                    act.wait_ge(gathered, 2 * b - 2)
                    act.wait_ge(onehot_dst, b)
                    stack_onehot(b, b % 2)

            def next_onehots(it):
                for s in range(2):
                    act.wait_ge(batch_loaded[s], 32 * it + 128)
                    act.wait_ge(gathered, 4 * it + (2 * s + 10))
                    act.wait_ge(onehot_dst, 2 * it + (s + 6))
                    stack_onehot(2 * it + (s + 6), s)

            with act.Fori(0, 3) as it:
                next_onehots(it)
            hi(1, 6, parts=(0,))
            with act.Fori(3, 6) as it:
                next_onehots(it)
            hi(1, 6, parts=(1,))
            with act.Fori(6, ET // 4 - 3) as it:
                next_onehots(it)

            def measure(a, i, s):
                nc.scalar.activation(distance[:, s, :], iota16[:], ACT.Abs, bias=idx_neg[:, a, bass.ds(i, 1)])\
                    .then_inc(distance_ready, 1)

            def source_rows(m):
                for pair in ((0, 1), (2, 3)):
                    for s in pair:
                        measure(0, 4 * m + s, s)
                    for s in pair:
                        act.wait_ge(distance_ready, 4 * m + s + 1)
                        nc.scalar.activation(oh_src[:, bass.ds(4 * m + s, 1), :].rearrange("p a n -> p (a n)"),
                                             distance[:, s, :], ACT.Relu, bias=1.0, scale=-1.0)\
                            .then_inc(src_act, 1)

            nc.scalar.activation(spare[:], row_no[:], ACT.Exp, scale=-1.0)
            act.wait_ge(seg_done, ET)
            with act.Fori(0, ACT_HEAD // 4) as m:
                source_rows(m)
            hi(0, 7)
            hi(1, 7)
            with act.Fori(ACT_HEAD // 4, ACT_TILES // 4 - 1) as m:
                source_rows(m)
            act.wait_ge(diff_ready, 1)
            nc.scalar.activation(ex[:], peak[:], ACT.Exp).then_inc(ex_ready, 1)
            act.wait_ge(ex_ready, 1)
            nc.scalar.activation(ex_16[:], ex[:], ACT.Copy).then_inc(ex_ready, 1)

            source_rows(ACT_TILES // 4 - 1)

            def destination_rows(m, b):
                i = OB * m + (OB - 1)
                measure(1, i, b)
                act.wait_ge(distance_ready, 2 * m + (ACT_TILES + 1))
                nc.scalar.activation(distance[:, b, :], distance[:, b, :], ACT.Relu, bias=1.0, scale=-1.0)\
                    .then_inc(distance_ready, 1)
                act.wait_ge(distance_ready, 2 * m + (ACT_TILES + 2))
                if not isinstance(m, int) or m:
                    act.wait_ge(paired, OB * m)
                for part, e in enumerate((ex_hi, ex_lo)):
                    last = nc.scalar.activation(oh_dst[:, OB - 1, part, :], distance[:, b, :], ACT.Identity,
                                                scale=e[:, bass.ds(i, 1)])
                last.then_inc(oh_act, 1)

            act.wait_ge(ex_split, 1)
            destination_rows(0, 0)
            destination_rows(1, 1)
            with act.Fori(1, ET // OB // 2) as m:
                for b in range(2):
                    destination_rows(2 * m + b, b)
            hi(0, 8, parts=(0,))
            act.wait_ge(paired, ET)
            nc.scalar.activation(pT[:], bank(4, 2).rearrange("p (t n) -> p t n", t=NT)[:, :, 0:N], ACT.Copy)\
                .then_inc(pT_ready, 1)
            hi(0, 8, parts=(1,))
            act.wait_ge(z_ready, 1)
            nc.scalar.activation(zT_hi[:, :, 0:NH], high_cn[:, :, 0:NH], ACT.Copy)
            nc.scalar.activation(zT_hi[:, :, 2 * NH:PADZ], high_cn[:, :, NH:N], ACT.Copy).then_inc(zhi_ready, 1)
            hi(1, 8)
            hi(0, 9)
            hi(1, 9)
            hi(0, SLOT_W, down=True, other=True)
            for t in range(NT):
                root(2 + t, t, t + 1)
            turn_hi(1)
            act.wait_ge(top_ready, 1)
            for t in range(NT):
                nc.scalar.activation(tope[:, t, 0:TOPK], tope[:, t, TOPK:2 * TOPK], ACT.Exp,
                                     accum_out=tsum[:, t, 0:1]).then_inc(tope_ready, 1)

            d_cols = bank(4, 2)
            t_cols = bank(6, 2)

            def silu(g):
                act.wait_ge(used[0], 2 * g + 2 * (SLOT_W + 1))
                nc.scalar.activation(act_g[:].rearrange("p t n -> p (t n)"), d_cols, ACT.Silu)\
                    .then_inc(silu_ready, 1)

            def gT_hi_part(g, to=gT_hi):
                act.wait_ge(gT_done, g + 1)
                nc.scalar.activation(to[:].rearrange("p b n -> p (b n)"), t_cols, ACT.Copy)\
                    .then_inc(gThi_ready, 1)

            hi(0, SLOT_W + 1, down=True, parts=(0,))
            silu(0)
            hi(0, SLOT_W + 1, down=True, parts=(1,))
            hi(1, SLOT_W)
            with act.Fori(1, NG - 1) as g:
                gT_hi_part(g - 1)
                silu(g)
                hi(0, g + (SLOT_W + 1), down=True)
                hi(1, g + SLOT_W)
            gT_hi_part(NG - 2)
            silu(NG - 1)
            hi(0, LAST, other=True)
            gT_hi_part(NG - 1, gT_last_hi)

        @block.vector
        def _(dve):
            links = [0]

            def link(ins):
                links[0] += 1
                ins.then_inc(chain, 1)
                dve.wait_ge(chain, links[0])

            def lo(s, n, down=False, parts=(0, 1)):
                for j in parts:
                    dve.wait_ge(hi_ready[s], 2 * n + (j + 1))
                    nc.vector.tensor_tensor(half(wlo, s, j, down), half(raw, s, j, down),
                                            half(whi, s, j, down).bitcast(F32), ALU.subtract)\
                        .then_inc(lo_ready[s], 1)

            def layer_norm(k, tiles, meanwhile=None):
                for t in tiles:
                    if k == 1:
                        dve.wait_ge(x_loaded[t], 16)
                    for j in range(2):
                        last = nc.vector.bn_stats(stats[:, t, j, :], xt[:, t, j * HALF:(j + 1) * HALF])
                link(last)
                for t in tiles:
                    last = nc.vector.bn_aggr(mv[:, t, :], stats[:, t, :, :].rearrange("p j s -> p (j s)"))
                link(last)
                var, root, inverse, other, rstd = (ln[:, q, tiles[0]:tiles[-1] + 1] for q in range(5))
                nc.vector.tensor_scalar(var, mv[:, tiles[0]:tiles[-1] + 1, 1], EPS, None, ALU.add)\
                    .then_inc(var_ready, 1)
                if meanwhile:
                    meanwhile()
                dve.wait_ge(root_ready, k)
                link(nc.vector.reciprocal(inverse, root))
                for t in tiles:
                    last = nc.vector.scalar_tensor_tensor(out=ln[:, 3, t:t + 1], in0=ln[:, 2, t:t + 1],
                                                          scalar=ln[:, 0, t:t + 1], in1=ln[:, 1, t:t + 1],
                                                          op0=ALU.mult, op1=ALU.add)
                link(last)
                link(nc.vector.tensor_scalar(inverse, other, 0.5, None, ALU.mult))
                link(nc.vector.reciprocal(rstd, inverse))
                for t in tiles:
                    nc.vector.tensor_scalar(nf[:, t, :], xt[:, t, :], mv[:, t, 0:1], ln[:, 4, t:t + 1],
                                            ALU.subtract, ALU.mult).then_inc(norm_ready, 1)

            def turn_lo(k):
                for t in range(NT):
                    dve.wait_ge(turned_hi, NT * k + t + 1)
                    for to, at, w in token_columns(k, t):
                        last = nc.vector.tensor_tensor(nT_lo[:, :, to:to + w], turned_cn[k][t][:, :, at:at + w],
                                                       nT_hi[:, :, to:to + w].bitcast(F32), ALU.subtract)
                    last.then_inc(turned_lo, 1)

            def pick():
                dve.wait_ge(consts, 6)
                dve.wait_ge(batch_loaded[0], 32)
                for a in range(2):
                    for j, number in enumerate((row_no[:, 0:1], node[:, 1:2])):
                        last = nc.vector.tensor_scalar(onehot[:, 1, 2 * a + j, 0:P], idx_b[:, 0, a, 0:P], number,
                                                       None, ALU.is_equal)
                last.then_inc(picker_ready, 1)

            layer_norm(1, range(NT), meanwhile=pick)
            dve.wait_ge(group_loaded, 16)
            ends = group_ends[:, 0:2]
            nc.vector.tensor_reduce(group_ends[:, 0:1], group_rows, mybir.AxisListType.X, ALU.min)
            link(nc.vector.tensor_reduce(group_ends[:, 1:2], group_rows, mybir.AxisListType.X, ALU.max))
            link(nc.vector.tensor_scalar(group_ends[:, 2:4], ends, float(NH), None, ALU.is_ge))
            for n in (2, 3):
                link(nc.vector.scalar_tensor_tensor(out=group_ends[:, 2 * n:2 * n + 2], in0=ends, scalar=float(n * NH),
                                                    in1=group_ends[:, 2 * n - 2:2 * n], op0=ALU.is_ge, op1=ALU.add))
            link(nc.vector.tensor_tensor(group_ends[:, 8:9], group_ends[:, 7:8], group_ends[:, 6:7], ALU.subtract))
            link(nc.vector.tensor_scalar(group_ends[:, 9:10], group_ends[:, 8:9], 2.0, 4.0, ALU.min, ALU.mult))
            nc.vector.tensor_tensor(group_ends[:, 10:11], group_ends[:, 9:10], group_ends[:, 6:7], ALU.add)
            dve.wait_ge(idx_loaded, 32)
            nc.vector.tensor_copy(idx_rowf[:], idx_rows[:]).then_inc(idx_float, 1)
            lo(0, 0)
            dve.wait_ge(bias_ready, 1)
            nc.vector.tensor_tensor(bias_lo[:], bias[:], bias_hi[:].bitcast(F32), ALU.subtract).then_inc(bias_ready, 1)
            for h in range(2):
                dve.wait_ge(feathi_ready, h + 1)
                both = slice(C * h, C * h + C)
                nc.vector.tensor_tensor(feat_lo[:, both, :].rearrange("p c e -> p (c e)"), bank(4 + 2 * h, 2),
                                        feat_hi[:, both, :].rearrange("p c e -> p (c e)").bitcast(F32),
                                        ALU.subtract).then_inc(featlo_ready, 1)
            lo(1, 0)
            turn_lo(0)
            dve.wait_ge(smallT, 1)
            nc.vector.tensor_copy(idx_col[:].rearrange("p a t -> p (a t)"), bank(4)[:, 0:2 * ET])
            nc.vector.tensor_scalar(idx_neg[:].rearrange("p a t -> p (a t)"), bank(4)[:, 0:2 * ET], -1.0, None,
                                    ALU.mult)
            nc.vector.tensor_copy(spans[:], bank(5)[0:1, 0:EG]).then_inc(small_ready, 1)
            lo(0, 1)
            lo(1, 1)
            lo(0, 2)

            def table_lo(k, h):
                for t in range(NT):
                    if h == 0:
                        dve.wait_ge(tabhi_ready, 6 * (k - 1) + t + 1)
                        nc.vector.tensor_tensor(tab_lo[:, t, :], bank(2 * t, 2), tab_hi[:, t, :].bitcast(F32),
                                                ALU.subtract).then_inc(tablo_ready, 1)
                    else:
                        for q in (2 * t, 2 * t + 1):
                            at = STACK_HI[q]
                            dve.wait_ge(tabhi_ready, 6 * (k - 1) + NT + q + 1)
                            nc.vector.tensor_tensor(tab_dst[NH - at:P - at, q, :], bank(4 + 2 * t, 2)[at:at + NH, :],
                                                    tab_dst[at:at + NH, q, :].bitcast(F32),
                                                    ALU.subtract).then_inc(tablo_ready, 1)

            def make_onehot(b, s, free=True):
                dve.wait_ge(batch_loaded[s], 32 * (b // 2 + 1))
                if free:
                    dve.wait_ge(gathered, 2 * b - 2)
                for j in range(NT):
                    last = nc.vector.tensor_scalar(onehot[:, s, j, :], idx_b[:, s, 0, :], node[:, j:j + 1], None,
                                                   ALU.is_equal)
                last.then_inc(onehot_ready, 1)

            def edge_tile(i, q):
                dve.wait_ge(gathered, i + 1)
                nc.vector.scalar_tensor_tensor(out=junk[:], in0=bank(2 * q, 2), scalar=0.0, in1=wa_b[:],
                                               op0=ALU.max, op1=ALU.mult,
                                               accum_out=logit[:, bass.ds(i, 1)]).then_inc(dot_done, 1)
                if not isinstance(i, int) or i:
                    dve.wait_ge(seg_done, i)
                nc.vector.tensor_scalar(pen[:], iota[:], idx_col[:, 1, bass.ds(i, 1)], NEVER,
                                        ALU.not_equal, ALU.mult).then_inc(pen_ready, 1)
                dve.wait_ge(pen_ready, i + 1)
                dve.wait_ge(dot_done, i + 1)
                nc.vector.scalar_tensor_tensor(out=segmax[:], in0=pen[:], scalar=logit[:, bass.ds(i, 1)],
                                               in1=segmax[:], op0=ALU.add, op1=ALU.max).then_inc(seg_done, 1)

            dve.wait_ge(consts, 14)
            make_onehot(0, 0, free=False)
            dve.wait_ge(feat_done, 2)
            make_onehot(1, 1, free=False)
            dve.wait_ge(small_ready, 1)
            dve.wait_ge(edge_loaded, 32)
            edge_tile(0, pair_of(0))
            for k in (1, 2):
                lo(1, 2 * k)
                lo(0, 2 * k + 1)
                table_lo(k, 0)
                lo(1, 2 * k + 1)
                lo(0, 2 * k + 2)
                table_lo(k, 1)
                for i in range(FIRST_TILE[k], min(FIRST_TILE[k + 1], 8)):
                    edge_tile(i, pair_of(i))
                    if i % 2 == 1:
                        make_onehot(i // 2 + 2, (i // 2) % 2)

            def loop_onehot(it, s):
                dve.wait_ge(batch_loaded[s], 32 * it + 128)
                dve.wait_ge(gathered, 4 * it + 2 * s + 10)
                for j in range(NT):
                    last = nc.vector.tensor_scalar(onehot[:, s, j, :], idx_b[:, s, 0, :], node[:, j:j + 1], None,
                                                   ALU.is_equal)
                last.then_inc(onehot_ready, 1)

            LOOPS = ET // 4 - 2
            with dve.Fori(0, LOOPS - 1) as it:
                for j in range(4):
                    edge_tile(4 * it + 8 + j, pair_of(8 + j))
                    if j % 2 == 1:
                        loop_onehot(it, j // 2)
            for i in range(ET - 4, ET):
                edge_tile(i, pair_of(i))
            dve.wait_ge(seg_done, ET)
            link(nc.vector.tensor_scalar(logit[:], logit[:], ba_b[:, 0:1], None, ALU.add))
            dve.wait_ge(segall_ready, 1)

            def edge_peak(i, s):
                nc.vector.scalar_tensor_tensor(out=junk2[:, s, :], in0=iota[:], scalar=idx_col[:, 1, bass.ds(i, 1)],
                                               in1=segall[:], op0=ALU.is_equal, op1=ALU.mult,
                                               accum_out=peak[:, bass.ds(i, 1)]).then_inc(peak_done, 1)

            for s in range(4):
                edge_peak(s, s)
            with dve.Fori(1, ET // 4) as i:
                for s in range(4):
                    dve.wait_ge(peak_done, 4 * i - 3 + s)
                    edge_peak(4 * i + s, s)
            dve.wait_ge(peak_done, ET)
            link(nc.vector.tensor_scalar(peak[:], peak[:], ba_b[:, 0:1], None, ALU.add))
            nc.vector.tensor_tensor(peak[:], logit[:], peak[:], ALU.subtract).then_inc(diff_ready, 1)
            dve.wait_ge(ex_ready, 2)
            link(nc.vector.tensor_copy(ex_hi[:], ex_16[:]))
            nc.vector.tensor_tensor(ex_lo[:], ex[:], ex_hi[:], ALU.subtract).then_inc(ex_split, 1)
            dve.wait_ge(ex_split, 1)

            def onehot_rows(i, s):
                for part, e in enumerate((ex_hi, ex_lo)):
                    last = nc.vector.tensor_scalar(oh_dst[:, s, part, :], iota16[:], idx_col[:, 1, bass.ds(i, 1)],
                                                   e[:, bass.ds(i, 1)], ALU.is_equal, ALU.mult)
                last.then_inc(oh_ready, 1)

            for s in range(OB - 1):
                onehot_rows(s, s)
            with dve.Fori(1, ET // OB) as i:
                for s in range(OB - 1):
                    dve.wait_ge(paired, OB * i + (s - OB + 1))
                    onehot_rows(OB * i + s, s)
            dve.wait_ge(den_ready, 1)
            link(nc.vector.tensor_scalar(rden[:], bank(6)[:, 0:N], 1e-30, None, ALU.max))
            link(nc.vector.reciprocal(rden[:], rden[:]))
            for t in range(NT):
                last = nc.vector.tensor_tensor(pT[:, t, :], pT[:, t, :], rden[:], ALU.mult)
            last.then_inc(pTn_ready, 1)
            dve.wait_ge(hash_turned, 1)
            nc.vector.tensor_copy(hashT[:].rearrange("p c w -> p (c w)"), bank(7)[:, 0:C * PD])
            nc.vector.tensor_copy(keysT[:], bank(7)[0:PD, XP:2 * XP]).then_inc(hash_ready, 1)
            lo(0, 8)
            dve.wait_ge(zhi_ready, 1)
            nc.vector.tensor_tensor(zT_lo[:, :, 0:NH], high_cn[:, :, 0:NH], zT_hi[:, :, 0:NH].bitcast(F32),
                                    ALU.subtract)
            nc.vector.tensor_tensor(zT_lo[:, :, 2 * NH:PADZ], high_cn[:, :, NH:N],
                                    zT_hi[:, :, 2 * NH:PADZ].bitcast(F32), ALU.subtract).then_inc(zlo_ready, 1)
            lo(1, 8)
            lo(0, 9)
            lo(1, 9)
            dve.wait_ge(x_again, 16)
            for t in range(NT):
                if t == 0:
                    dve.wait_ge(nodes_done, 1)
                else:
                    dve.wait_ge(used[1], 2 * SLOT_W)
                nc.vector.scalar_tensor_tensor(out=xt[:, t, :], in0=bank(2 * t, 2), scalar=0.0,
                                               in1=xt[:, t, :], op0=ALU.max, op1=ALU.add).then_inc(x2_ready, 1)
                dve.wait_ge(x2_ready, t + 1)
                layer_norm(2 + t, (t,))
            turn_lo(1)

            dve.wait_ge(hT_done, 1)
            nc.vector.tensor_copy(hT_sb[:], bank(1)[0:PD, 0:N]).then_inc(hT_copied, 1)
            dve.wait_ge(sim_done, 1)
            link(nc.vector.tensor_copy(sim[:], bank(2).rearrange("p (t n) -> p t n", t=NT)))
            for t in range(NT):
                last = nc.vector.max(top[:, t, :], sim[:, t, :])
            link(last)
            for t in range(NT):
                nc.vector.tensor_scalar(tope[:, t, TOPK:2 * TOPK], top[:, t, 0:TOPK], top[:, t, 0:1], None,
                                        ALU.subtract)
                last = nc.vector.max_index(topi[:, t, :], top[:, t, :], sim[:, t, :])
            last.then_inc(top_ready, 1)
            dve.wait_ge(top_ready, 1)
            link(nc.vector.tensor_copy(topf[:], topi[:]))
            dve.wait_ge(tope_ready, NT)
            link(nc.vector.reciprocal(tsum[:, :, 1], tsum[:, :, 0]))
            for t in range(NT):
                link(nc.vector.tensor_scalar(tope[:, t, 0:TOPK], tope[:, t, 0:TOPK], tsum[:, t, 1:2], None, ALU.mult))
                link(nc.vector.tensor_scalar(route[:, t, :], iota[:], topf[:, t, 0:1], tope[:, t, 0:1],
                                             ALU.is_equal, ALU.mult))
                for k in range(1, TOPK):
                    link(nc.vector.tensor_scalar(rtmp[:, t, :], iota[:], topf[:, t, k:k + 1], tope[:, t, k:k + 1],
                                                 ALU.is_equal, ALU.mult))
                    link(nc.vector.tensor_tensor(route[:, t, :], route[:, t, :], rtmp[:, t, :], ALU.add))

            def weigh(g):
                dve.wait_ge(silu_ready, g + 1)
                for t in range(NT):
                    w = route[:, t, bass.ds(g * GX, GX)].unsqueeze(2).to_broadcast([P, GX, PD])
                    last = nc.vector.tensor_tensor(gw[:, t, :].rearrange("p (n w) -> p n w", n=GX),
                                                   act_g[:, t, :].rearrange("p (n w) -> p n w", n=GX), w, ALU.mult)
                last.then_inc(gw_ready, 1)

            def gT_lo_part(g, to=gT_lo, part_hi=gT_hi):
                dve.wait_ge(gThi_ready, g + 1)
                nc.vector.tensor_tensor(to[:].rearrange("p b n -> p (b n)"), bank(6, 2),
                                        part_hi[:].rearrange("p b n -> p (b n)").bitcast(F32), ALU.subtract)\
                    .then_inc(gTlo_ready, 1)

            weigh(0)
            dve.wait_ge(lo_ready[0], 2 * (SLOT_W + 1) + 1)
            lo(0, SLOT_W + 1, down=True, parts=(1,))
            for t in range(NT):
                nc.vector.tensor_tensor(xt[:, t, :], xt[:, t, :], nf[:, t, :], ALU.add)
            lo(1, SLOT_W)
            with dve.Fori(1, NG - 1) as g:
                gT_lo_part(g - 1)
                weigh(g)
                lo(0, g + (SLOT_W + 1), down=True)
                lo(1, g + SLOT_W)
            gT_lo_part(NG - 2)
            weigh(NG - 1)
            lo(0, LAST)
            gT_lo_part(NG - 1, gT_last_lo, gT_last_hi)
            for n in range(2 * NT):
                t, cols = n // 2, slice((n % 2) * HALF, (n % 2 + 1) * HALF)
                dve.wait_ge(summed, n + 1)
                nc.vector.scalar_tensor_tensor(out=xt[:, t, cols], in0=bank(n), scalar=scale_b[:, 0:1],
                                               in1=xt[:, t, cols], op0=ALU.mult, op1=ALU.add).then_inc(out_ready, 1)

        @block.tensor
        def _(pe):
            def transpose(o, i):
                k = i.shape[0]
                return nc.tensor.transpose(o, i, ident[0:k, 0:k])

            def turn(k):
                for t in range(NT):
                    pe.wait_ge(norm_ready, k * NT + t + 1)
                    for c in range(C):
                        last = transpose(turned_cn[k][t][:, c, :],
                                         nf[:, t, :].rearrange("p (q c) -> p c q", c=C)[:, c, :])
                    last.then_inc(turned, 1)

            pe.wait_ge(consts, 6)
            pe.wait_ge(norm_ready, NT)
            pe.wait_ge(picker_ready, 1)
            for h in range(2):
                for c in range(C):
                    for t in range(NT):
                        last = nc.tensor.matmul(bank(4 + 2 * h, 2)[:, c * P:(c + 1) * P],
                                                nf[:, t, :].rearrange("p (q c) -> p c q", c=C)[:, c, :],
                                                onehot[:, 1, 2 * h + t, 0:P].bitcast(F32),
                                                start=t == 0, stop=t == NT - 1)
                last.then_inc(feat_done, 1)
            turn(0)
            pe.wait_ge(idx_float, 1)
            pe.wait_ge(featlo_ready, 1)
            for a in range(2):
                transpose(bank(4)[:, a * ET:(a + 1) * ET], idx_rowf[:, a, :])
            transpose(bank(5)[0:1, 0:EG], group_ends[:, 10:11]).then_inc(smallT, 1)

            def three(o, a_hi, a_lo, b_hi, b_lo, start, stop):
                nc.tensor.matmul(o, a_hi, b_hi, start=start, stop=False)
                nc.tensor.matmul(o, a_lo, b_hi, start=False, stop=False)
                return nc.tensor.matmul(o, a_hi, b_lo, start=False, stop=stop)

            def add_bias(o, rows, g, start=True, stop=False):
                cols = slice(g * HALF, (g + 1) * HALF)
                nc.tensor.matmul(o, rows, bias_hi[:, cols], start=start, stop=False)
                return nc.tensor.matmul(o, rows, bias_lo[:, cols], start=False, stop=stop)

            w_hi = [whi[:, s, :].rearrange("p (c n) -> p c n", c=4) for s in range(2)]
            w_lo = [wlo[:, s, :].rearrange("p (c n) -> p c n", c=4) for s in range(2)]

            def gather(q, s, odd, stacks=(0, 1, 2, 3), first=None):
                edges = slice(odd * P, (odd + 1) * P)
                for t in range(NT):
                    if first is not None:
                        pe.wait_ge(tablo_ready, 6 * (first - 1) + t + 1)
                    for h in range(2):
                        for part, tab in enumerate((tab_hi, tab_lo)):
                            nc.tensor.matmul(bank(2 * q + h), onehot[:, s, t, edges],
                                             tab[:, t, h * HALF:(h + 1) * HALF],
                                             start=t == 0 and part == 0, stop=False)
                for n in stacks:
                    if first is not None:
                        pe.wait_ge(tablo_ready, 6 * (first - 1) + NT + n + 1)
                    for h in range(2):
                        last = nc.tensor.matmul(bank(2 * q + h), onehot[:, s, 2 + n, edges],
                                                tab_dst[:, n, h * HALF:(h + 1) * HALF],
                                                start=False, stop=n == stacks[-1])
                last.then_inc(gathered, 1)

            def project(k, h):
                if h == 1:
                    for t in range(NT):
                        for g in range(2):
                            add_bias(bank(4 + 2 * t + g), sel[:, k, :], g)

                def add(c, t):
                    s, cc = c // 4, c % 4
                    for g in range(2):
                        last = three(bank(4 * h + 2 * t + g), tokens(nT_hi, c, t), tokens(nT_lo, c, t),
                                     w_hi[s][:, cc, g * HALF:(g + 1) * HALF],
                                     w_lo[s][:, cc, g * HALF:(g + 1) * HALF],
                                     start=h == 0 and c == 0, stop=c == C - 1)
                    return last

                def ready(c):
                    if c % 2 == 0:
                        pe.wait_ge(lo_ready[c // 4], 2 * (2 * k + h) + (c % 4) // 2 + 1)

                together = C if h == 0 else C // 2
                for c in range(together):
                    ready(c)
                    for t in range(NT):
                        last = add(c, t)
                        if c == C - 1 and t == 0:
                            last.then_inc(table_done, 1)
                    if c % 2 == 1:
                        last.then_inc(used[c // 4], 1)
                for t in range(NT):
                    for c in range(together, C):
                        if t == 0:
                            ready(c)
                        last = add(c, t)
                        if c == C - 1 and t == 0:
                            last.then_inc(table_done, 1)
                        if c % 2 == 1 and t == 1:
                            last.then_inc(used[1], 1)

            pe.wait_ge(consts, 14)
            pe.wait_ge(bias_ready, 2)
            pe.wait_ge(featlo_ready, 2)
            for h in range(2):
                for s in range(2):
                    for cc in range(4):
                        if cc % 2 == 0:
                            pe.wait_ge(lo_ready[s], 2 * h + cc // 2 + 1)
                        c = 4 * s + cc
                        for g in range(2):
                            last = three(bank(6 + g), feat_hi[:, C * h + c, :], feat_lo[:, C * h + c, :],
                                         w_hi[s][:, cc, g * HALF:(g + 1) * HALF],
                                         w_lo[s][:, cc, g * HALF:(g + 1) * HALF],
                                         start=h == 0 and c == 0, stop=False)
                        if cc % 2 == 1:
                            last.then_inc(used[s], 1)
            for g in range(2):
                last = add_bias(bank(6 + g), sel[:, 0, :], g, start=False, stop=True)
            last.then_inc(gathered, 1)

            pe.wait_ge(turned_lo, NT)
            pe.wait_ge(small_ready, 1)
            for k in (1, 2):
                if k == 2:
                    pe.wait_ge(dot_done, 3)
                project(k, 0)
                pe.wait_ge(dot_done, FIRST_TILE[k])
                project(k, 1)
                for i in range(FIRST_TILE[k], min(FIRST_TILE[k + 1], 2 * GROUP)):
                    pe.wait_ge(onehot_ready, i // 2 + 1)
                    pe.wait_ge(onehot_dst, i // 2 + 1)
                    if i >= 4:
                        pe.wait_ge(dot_done, i - 1 if i == FIRST_TILE[2] - 1 else i - 3)
                    gather(pair_of(i), (i // 2) % 2, i % 2, first=k if i == FIRST_TILE[k] else None)

            def gather_group(it, stacks):
                for j in range(GROUP):
                    pe.wait_ge(onehot_ready, 2 * it + 5 + j // 2)
                    pe.wait_ge(onehot_dst, 2 * it + 5 + j // 2)
                    pe.wait_ge(dot_done, 4 * it + 5 + j)
                    gather(pair_of(2 * GROUP + j), j // 2, j % 2, stacks)

            with pe.Fori(0, EG - 2) as it:
                span = pe.value_load(spans[0:1, bass.ds(it + 2, 1)], min_val=0, max_val=9)
                for number, stacks in enumerate(SPANS):
                    with pe.If(span == number):
                        gather_group(it, stacks)
                with pe.If(span >= len(SPANS)):
                    gather_group(it, (0, 1, 2, 3))

            pe.wait_ge(dot_done, ET)
            sel_cols = sel[:].rearrange("q b n -> q (b n)")
            for t, first in enumerate((3 * P + NH, 4 * P)):
                for g in range(2):
                    add_bias(bank(2 * t + g), sel_cols[:, first:first + P], g)

            def new_nodes(aT_hi, aT_lo, columns, u, first_kind, stop=False, parts=(0, 1)):
                s = u % 2
                tiles = tuple(enumerate(columns[:1] if first_kind else columns[1:]))

                def add(t, at, j):
                    for c in (4 * s + 2 * j, 4 * s + 2 * j + 1):
                        for g in range(2):
                            last = three(bank(2 * t + g), aT_hi[:, c, at:at + P], aT_lo[:, c, at:at + P],
                                         w_hi[s][:, c % 4, g * HALF:(g + 1) * HALF],
                                         w_lo[s][:, c % 4, g * HALF:(g + 1) * HALF],
                                         start=False, stop=stop and c == C - 1)
                    return last

                if stop:
                    for t, at in tiles:
                        for j in parts:
                            if t == 0:
                                pe.wait_ge(lo_ready[s], 2 * (u // 2) + j + 1)
                            last = add(t, at, j)
                            if t == 1:
                                last.then_inc(used[s], 1)
                        if t == 0:
                            last.then_inc(nodes_done, 1)
                    return
                for j in parts:
                    pe.wait_ge(lo_ready[s], 2 * (u // 2) + j + 1)
                    for t, at in tiles:
                        last = add(t, at, j)
                    last.then_inc(used[s], 1)

            own = (2 * NH, 0, 4 * NH)
            messages = (0, NH, 3 * NH)
            new_nodes(nT_hi, nT_lo, own, 12, True)
            new_nodes(nT_hi, nT_lo, own, 13, True)
            new_nodes(nT_hi, nT_lo, own, 14, False)
            new_nodes(nT_hi, nT_lo, own, 15, False, parts=(0,))

            def pair(m, s, start=False, stop=False):
                if s == OB - 1:
                    pe.wait_ge(oh_act, m + 1)
                else:
                    pe.wait_ge(oh_ready, (OB - 1) * m + s + 1)
                rows = oh_src[:, bass.ds(OB * m + s, 1), :].rearrange("p a n -> p (a n)")
                for t in range(NT):
                    for part in range(2):
                        last = nc.tensor.matmul(bank(4 + t)[:, 0:N], rows[:, t * P:(t + 1) * P],
                                                oh_dst[:, s, part, :], start=start and part == 0,
                                                stop=stop and part == 1)
                last.then_inc(paired, 1)

            pe.wait_ge(src_act, OB)
            for s in range(OB):
                pair(0, s, start=s == 0)
            with pe.Fori(1, ACT_TILES // OB) as m:
                pe.wait_ge(src_act, OB * m + OB)
                for s in range(OB):
                    pair(m, s)
            with pe.Fori(ACT_TILES // OB, ET // OB - 1) as m:
                pe.wait_ge(src_pool, OB * m + (OB - ACT_TILES))
                for s in range(OB):
                    pair(m, s)
            pe.wait_ge(src_pool, POOL_TILES)
            for s in range(OB):
                pair(ET // OB - 1, s, stop=s == OB - 1)
            pe.wait_ge(pT_ready, 1)
            pe.wait_ge(pool_chain, 3)
            for t in range(NT):
                last = nc.tensor.matmul(bank(6)[:, 0:N], ones[:], pT[:, t, :], start=t == 0, stop=t == NT - 1)
            last.then_inc(den_ready, 1)
            pe.wait_ge(hash_loaded, 32)
            for c in range(C):
                transpose(bank(7)[:, c * PD:(c + 1) * PD], hash_w[:].rearrange("w (q c) -> w c q", c=C)[:, c, :])
            for t in range(NT):
                last = transpose(bank(7)[0:PD, XP + t * P:XP + (t + 1) * P], keys_n[:, t, :])
            last.then_inc(hash_turned, 1)
            pe.wait_ge(pTn_ready, 1)
            for c in range(C):
                if c == C - 2:
                    pe.wait_ge(hash_ready, 1)
                for t in range(NT):
                    last = nc.tensor.matmul(high_cn[:, c, :], nf[:, t, :].rearrange("p (q c) -> p c q", c=C)[:, c, :],
                                            pT[:, t, :], start=t == 0, stop=t == NT - 1)
            last.then_inc(z_ready, 1)
            new_nodes(nT_hi, nT_lo, own, 15, False, parts=(1,))
            pe.wait_ge(zlo_ready, 1)
            pe.wait_ge(z_zeroed, 2)
            new_nodes(zT_hi, zT_lo, messages, 16, True)
            new_nodes(zT_hi, zT_lo, messages, 17, True)
            new_nodes(zT_hi, zT_lo, messages, 18, False)
            new_nodes(zT_hi, zT_lo, messages, 19, False, stop=True)

            turn(1)
            for part, (aT, there) in enumerate(((nT_hi, turned_hi), (nT_lo, turned_lo))):
                pe.wait_ge(there, 2 * NT)
                for c in range(C):
                    last = nc.tensor.matmul(bank(1)[0:PD, 0:N], hashT[:, c, :], aT[:, c, 2 * NH:PADN].bitcast(F32),
                                            start=c == 0 and part == 0, stop=c == C - 1 and part == 1)
            last.then_inc(hT_done, 1)
            pe.wait_ge(hT_copied, 1)
            for t in range(NT):
                last = nc.tensor.matmul(bank(2)[:, t * N:(t + 1) * N], hT_sb[:, t * P:(t + 1) * P], keysT[:],
                                        start=True, stop=True)
            last.then_inc(sim_done, 1)

            down_hi = whi[:, 0, :].rearrange("p (n c w) -> p c n w", n=GX, c=C)
            down_lo = wlo[:, 0, :].rearrange("p (n c w) -> p c n w", n=GX, c=C)

            def down(g):
                for c in range(C):
                    if c % 4 == 0:
                        pe.wait_ge(lo_ready[0], 2 * g + (2 * SLOT_W + c // 4 + 1))
                    for t in range(NT):
                        cols = slice((2 + 2 * t) * NH, (4 + 2 * t) * NH)
                        last = three(bank(4 + t), nT_hi[:, c, cols], nT_lo[:, c, cols],
                                     down_hi[:, c, :, :], down_lo[:, c, :, :], start=c == 0, stop=c == C - 1)
                    if c % 4 == 3:
                        last.then_inc(used[0], 1)

            def turn_group(g):
                pe.wait_ge(gw_ready, g + 1)
                for b in range(BLOCKS):
                    for t in range(NT):
                        last = transpose(ps[:, 6 * HALF + b * N + t * P:6 * HALF + b * N + (t + 1) * P],
                                         gw[:, t, b * P:(b + 1) * P])
                last.then_inc(gT_done, 1)

            def up_block(s, b, t, h, aT_hi, aT_lo, stop=False):
                return three(bank(2 * t + h), aT_hi[:, b, t * P:(t + 1) * P], aT_lo[:, b, t * P:(t + 1) * P],
                             w_hi[s][:, b, h * HALF:(h + 1) * HALF], w_lo[s][:, b, h * HALF:(h + 1) * HALF],
                             start=False, stop=stop)

            def up(g, part):
                pe.wait_ge(lo_ready[1], 2 * g + (2 * SLOT_W + part + 1))
                for b in (2 * part, 2 * part + 1):
                    for t in range(NT):
                        for h in range(2):
                            last = up_block(1, b, t, h, gT_hi, gT_lo)
                last.then_inc(used[1], 1)

            down(0)
            pe.wait_ge(top_ready, 1)
            for b in range(4):
                nc.tensor.matmul(bank(b), sel[0:1, 1, :], sel_cols[0:1, P:P + HALF], start=True, stop=False)
            turn_group(0)
            with pe.Fori(1, NG - 1) as g:
                pe.wait_ge(silu_ready, g)
                down(g)
                pe.wait_ge(gTlo_ready, g)
                for part in range(2):
                    up(g - 1, part)
                turn_group(g)
            pe.wait_ge(silu_ready, NG - 1)
            down(NG - 1)
            pe.wait_ge(gTlo_ready, NG - 1)
            up(NG - 2, 0)
            turn_group(NG - 1)
            up(NG - 2, 1)
            pe.wait_ge(gTlo_ready, NG)
            pe.wait_ge(lo_ready[0], 2 * LAST + 2)
            for t in range(NT):
                for h in range(2):
                    for b in range(BLOCKS):
                        last = up_block(0, b, t, h, gT_last_hi, gT_last_lo, stop=b == BLOCKS - 1)
                    last.then_inc(summed, 1)


_INS = ['x', 'src', 'dst', 'L0_gnn_W_hh', 'L0_gnn_b_hh', 'L0_gnn_W_oo', 'L0_gnn_b_oo', 'L0_gnn_W_ho', 'L0_gnn_b_ho',
        'L0_gnn_W_a', 'L0_gnn_b_a', 'L0_gnn_W_hn', 'L0_gnn_b_hn', 'L0_gnn_W_on', 'L0_gnn_b_on', 'L0_ffn_hasher_w',
        'L0_ffn_keys', 'L0_ffn_values_down', 'L0_ffn_values_up', 'L0_ffn_scale']


def kernel(**inputs):
    import numpy as _np
    import concourse.bacc as _bacc
    from concourse import mybir as _mybir
    from concourse.bass_utils import run_bass_kernel_spmd as _run

    nc = _bacc.Bacc("TRN2", target_bir_lowering=False, num_devices=1)
    arrays, args = {}, []
    for name in _INS:
        a = _np.ascontiguousarray(inputs[name])
        arrays[f"in_{name}_dram"] = a
        args.append(nc.dram_tensor(f"in_{name}_dram", a.shape, _mybir.dt.from_np(a.dtype), kind="ExternalInput").ap())
    out = nc.dram_tensor("out_0_dram", (N, D), _mybir.dt.float32, kind="ExternalOutput").ap()
    gnn_ffn(nc, *args, out)
    r = _run(nc, [arrays], core_ids=[0])
    return r.results[0]["out_0_dram"]
```
